# Optimizing a Trainium2 kernel written in Bass

```python
import numpy as np
import jax
import jax.numpy as jnp

def _softmax(x, axis=-1):
    return jax.nn.softmax(x, axis=axis)

def _gelu(x):
    return jax.nn.gelu(x, approximate=True)

def _silu(x):
    return jax.nn.silu(x)

def _sigmoid(x):
    return jax.nn.sigmoid(x)

def _layernorm(x, axis=-1, eps=1e-05):
    m = jnp.mean(x, axis=axis, keepdims=True)
    v = jnp.var(x, axis=axis, keepdims=True)
    return (x - m) / jnp.sqrt(v + eps)

def _scatter_add(tgt, idx, src, axis=0):
    return tgt.at[idx].add(src)

def _segment_sum(src, seg, n):
    return jax.ops.segment_sum(src, seg, n)
kernel_name = 'mk_decoder_postln_d1_seqx_r8_54f964'

def setup_inputs(seed: int=0):
    np.random.seed(seed)
    _w = jnp.asarray

    def _rec_inputs():
        import jax
        import jax.numpy as jnp
        _rk = jax.random.key(seed)
        x = -0.0005207 + 1.001 * jax.random.normal(jax.random.fold_in(_rk, 1), (8, 128, 512), jnp.float32)
        _lenS = 128 - jax.random.randint(jax.random.fold_in(_rk, 7), (8,), 0, max(1, 128 // 4) + 1, jnp.int32)
        _lenS2 = 128 - jax.random.randint(jax.random.fold_in(_rk, 8), (8,), 0, max(1, 128 // 4) + 1, jnp.int32)
        _ctx_4096P = jax.random.normal(jax.random.fold_in(_rk, 11), (8, 16, 512), jnp.float32)
        _ctx_4096c = jax.random.dirichlet(jax.random.fold_in(_rk, 511), 0.3 * jnp.ones((16,), jnp.float32), (8, 128))
        _ctx_4096t = jnp.einsum('bsk,bkd->bsd', _ctx_4096c, _ctx_4096P)
        _ctx_4096t = _ctx_4096t * jax.lax.rsqrt(jnp.mean(jnp.square(_ctx_4096t)) + 1e-12) * 0.953939
        ctx_4096 = -0.00010331 + 0.999899 * (_ctx_4096t + 0.3 * jax.random.normal(jax.random.fold_in(_rk, 611), (8, 128, 512), jnp.float32))
        return (x, ctx_4096)
    x, ctx_4096 = _rec_inputs()

    def _L0_attn_setup():
        import jax, jax.numpy as jnp
        import numpy as np
        import math
        NH, NKV, D = (32, 8, 128)

        def _alibi_slopes(n):
            cp2 = 2 ** math.floor(math.log2(n))
            base = 2.0 ** (-8.0 / cp2)
            slopes = base ** np.arange(1, cp2 + 1, dtype=np.float32)
            if cp2 != n:
                extra_base = 2.0 ** (-4.0 / cp2)
                extra = extra_base ** np.arange(1, 1 + 2 * (n - cp2), 2, dtype=np.float32)
                slopes = np.concatenate([slopes, extra])
            return slopes.astype(np.float32)
        key = jax.random.key(seed)
        k1, k2, k3 = jax.random.split(key, 3)
        B, S, H = (4, 128, 512)
        qkv_out = NH * D + 2 * NKV * D
        return {'hidden_states': jax.random.normal(k1, (B, S, H), jnp.float32) * 0.02, 'w_qkv': jax.random.normal(k2, (H, qkv_out), jnp.float32) * 0.02, 'w_o': jax.random.normal(k3, (NH * D, H), jnp.float32) * 0.02}
    _L0_attn_all = _L0_attn_setup()
    _L0_attn_in = {k: v for k, v in _L0_attn_all.items() if k in ('w_qkv', 'w_o')}
    del _L0_attn_all

    def _L0_xattn_setup():
        import jax, jax.numpy as jnp
        import numpy as np
        HEADS = 32
        KV_HEADS = 8
        HEAD_DIM = 128
        EPS = 1e-06

        def rms_norm(x, w):
            var = jnp.mean(jnp.square(x.astype(jnp.float32)), axis=-1, keepdims=True)
            return (x.astype(jnp.float32) * jax.lax.rsqrt(var + EPS)).astype(x.dtype) * w
        key = jax.random.key(seed)
        ks = jax.random.split(key, 6)
        bsz, n_lat, seq, hidden = (8, 64, 512, 512)
        return {'latents': jax.random.normal(ks[0], (bsz, n_lat, hidden), jnp.float32), 'context': jax.random.normal(ks[1], (bsz, seq, hidden), jnp.float32), 'Wq': jax.random.normal(ks[2], (hidden, HEADS * HEAD_DIM), jnp.float32) * 0.02, 'Wk': jax.random.normal(ks[3], (hidden, KV_HEADS * HEAD_DIM), jnp.float32) * 0.02, 'Wv': jax.random.normal(ks[4], (hidden, KV_HEADS * HEAD_DIM), jnp.float32) * 0.02, 'Wo': jax.random.normal(ks[5], (HEADS * HEAD_DIM, hidden), jnp.float32) * 0.02, 'q_norm_w': jnp.ones((HEAD_DIM,), jnp.float32), 'k_norm_w': jnp.ones((HEAD_DIM,), jnp.float32)}
    _L0_xattn_all = _L0_xattn_setup()
    _L0_xattn_in = {k: v for k, v in _L0_xattn_all.items() if k in ('Wq', 'Wk', 'Wv', 'Wo', 'q_norm_w', 'k_norm_w')}
    del _L0_xattn_all

    def _L0_ffn_setup():
        import jax, jax.numpy as jnp
        import numpy as np
        LORA_SCALING = 1.0 / 2.0

        def _qlora_linear(x, wq, A, B):
            w = jnp.tile(wq, (1, 4))
            base = x @ w.T
            lora = x @ A.T @ B.T
            return base + lora * LORA_SCALING
        key = jax.random.key(seed)
        ks = jax.random.split(key, 10)
        d, h, r = (512, 1376, 2)
        return {'x': jax.random.normal(ks[0], (16, 1, d), dtype=jnp.float32), 'w1q': jax.random.normal(ks[1], (h, d // 4), dtype=jnp.float32) * 0.02, 'a1': jax.random.normal(ks[2], (r, d), dtype=jnp.float32) * 0.02, 'b1': jax.random.normal(ks[3], (h, r), dtype=jnp.float32) * 0.02, 'w3q': jax.random.normal(ks[4], (h, d // 4), dtype=jnp.float32) * 0.02, 'a3': jax.random.normal(ks[5], (r, d), dtype=jnp.float32) * 0.02, 'b3': jax.random.normal(ks[6], (h, r), dtype=jnp.float32) * 0.02, 'w2q': jax.random.normal(ks[7], (d, h // 4), dtype=jnp.float32) * 0.02, 'a2': jax.random.normal(ks[8], (r, h), dtype=jnp.float32) * 0.02, 'b2': jax.random.normal(ks[9], (d, r), dtype=jnp.float32) * 0.02}
    _L0_ffn_all = _L0_ffn_setup()
    _L0_ffn_in = {k: v for k, v in _L0_ffn_all.items() if k in ('w1q', 'a1', 'b1', 'w3q', 'a3', 'b3', 'w2q', 'a2', 'b2')}
    del _L0_ffn_all
    return {'x': x, 'ctx_4096': ctx_4096, 'L0_attn_w_qkv': _L0_attn_in['w_qkv'], 'L0_attn_w_o': _L0_attn_in['w_o'], 'L0_xattn_Wq': _L0_xattn_in['Wq'], 'L0_xattn_Wk': _L0_xattn_in['Wk'], 'L0_xattn_Wv': _L0_xattn_in['Wv'], 'L0_xattn_Wo': _L0_xattn_in['Wo'], 'L0_xattn_q_norm_w': _L0_xattn_in['q_norm_w'], 'L0_xattn_k_norm_w': _L0_xattn_in['k_norm_w'], 'L0_ffn_w1q': _L0_ffn_in['w1q'], 'L0_ffn_a1': _L0_ffn_in['a1'], 'L0_ffn_b1': _L0_ffn_in['b1'], 'L0_ffn_w3q': _L0_ffn_in['w3q'], 'L0_ffn_a3': _L0_ffn_in['a3'], 'L0_ffn_b3': _L0_ffn_in['b3'], 'L0_ffn_w2q': _L0_ffn_in['w2q'], 'L0_ffn_a2': _L0_ffn_in['a2'], 'L0_ffn_b2': _L0_ffn_in['b2']}

def reference(x, ctx_4096, L0_attn_w_qkv, L0_attn_w_o, L0_xattn_Wq, L0_xattn_Wk, L0_xattn_Wv, L0_xattn_Wo, L0_xattn_q_norm_w, L0_xattn_k_norm_w, L0_ffn_w1q, L0_ffn_a1, L0_ffn_b1, L0_ffn_w3q, L0_ffn_a3, L0_ffn_b3, L0_ffn_w2q, L0_ffn_a2, L0_ffn_b2):
    import jax
    import jax.numpy as jnp

    def _L0_attn_ref(hidden_states, w_qkv, w_o):
        import jax, jax.numpy as jnp
        import numpy as np
        import math
        NH, NKV, D = (32, 8, 128)

        def _alibi_slopes(n):
            cp2 = 2 ** math.floor(math.log2(n))
            base = 2.0 ** (-8.0 / cp2)
            slopes = base ** np.arange(1, cp2 + 1, dtype=np.float32)
            if cp2 != n:
                extra_base = 2.0 ** (-4.0 / cp2)
                extra = extra_base ** np.arange(1, 1 + 2 * (n - cp2), 2, dtype=np.float32)
                slopes = np.concatenate([slopes, extra])
            return slopes.astype(np.float32)
        B, S, H = hidden_states.shape
        G = NH // NKV
        scale = D ** (-0.5)
        qkv = hidden_states @ w_qkv
        q = qkv[..., :NH * D].reshape(B, S, NKV, G, D)
        k = qkv[..., NH * D:NH * D + NKV * D].reshape(B, S, NKV, D)
        v = qkv[..., NH * D + NKV * D:].reshape(B, S, NKV, D)
        scores = jnp.einsum('bqhgd,bkhd->bhgqk', q, k) * scale
        slopes = jnp.asarray(_alibi_slopes(NH)).reshape(NKV, G)
        pos = jnp.arange(S)
        rel = pos[:, None] - pos[None, :]
        sqrt_dist = jnp.sqrt(jnp.maximum(rel, 0).astype(jnp.float32))
        bias = -slopes[:, :, None, None] * sqrt_dist
        bias = jnp.where(rel[None, None] >= 0, bias, -jnp.inf)
        attn = jax.nn.softmax(scores + bias[None], axis=-1)
        out = jnp.einsum('bhgqk,bkhd->bqhgd', attn, v).reshape(B, S, NH * D)
        return out @ w_o

    def _L0_xattn_ref(latents, context, Wq, Wk, Wv, Wo, q_norm_w, k_norm_w):
        import jax, jax.numpy as jnp
        import numpy as np
        HEADS = 32
        KV_HEADS = 8
        HEAD_DIM = 128
        EPS = 1e-06

        def rms_norm(x, w):
            var = jnp.mean(jnp.square(x.astype(jnp.float32)), axis=-1, keepdims=True)
            return (x.astype(jnp.float32) * jax.lax.rsqrt(var + EPS)).astype(x.dtype) * w
        bsz, q_len, hidden = latents.shape
        kv = jnp.concatenate([context, latents], axis=1)
        kv_len = kv.shape[1]
        groups = HEADS // KV_HEADS
        q = (latents @ Wq).reshape(bsz, q_len, HEADS, HEAD_DIM).transpose(0, 2, 1, 3)
        k = (kv @ Wk).reshape(bsz, kv_len, KV_HEADS, HEAD_DIM).transpose(0, 2, 1, 3)
        v = (kv @ Wv).reshape(bsz, kv_len, KV_HEADS, HEAD_DIM).transpose(0, 2, 1, 3)
        q = rms_norm(q, q_norm_w)
        k = rms_norm(k, k_norm_w)
        qg = q.reshape(bsz, KV_HEADS, groups, q_len, HEAD_DIM)
        scale = 1.0 / np.sqrt(HEAD_DIM)
        scores = jnp.einsum('bhgqd,bhkd->bhgqk', qg, k) * scale
        probs = jax.nn.softmax(scores.astype(jnp.float32), axis=-1).astype(q.dtype)
        out = jnp.einsum('bhgqk,bhkd->bhgqd', probs, v)
        out = out.reshape(bsz, HEADS, q_len, HEAD_DIM).transpose(0, 2, 1, 3)
        out = out.reshape(bsz, q_len, HEADS * HEAD_DIM)
        return out @ Wo

    def _L0_ffn_ref(x, w1q, a1, b1, w3q, a3, b3, w2q, a2, b2):
        import jax, jax.numpy as jnp
        import numpy as np
        LORA_SCALING = 1.0 / 2.0

        def _qlora_linear(x, wq, A, B):
            w = jnp.tile(wq, (1, 4))
            base = x @ w.T
            lora = x @ A.T @ B.T
            return base + lora * LORA_SCALING
        gate = jax.nn.silu(_qlora_linear(x, w1q, a1, b1))
        up = _qlora_linear(x, w3q, a3, b3)
        return _qlora_linear(gate * up, w2q, a2, b2)
    x = _layernorm(x + _L0_attn_ref(x, L0_attn_w_qkv, L0_attn_w_o), axis=-1)
    x = _layernorm(x + _L0_xattn_ref(x, ctx_4096, L0_xattn_Wq, L0_xattn_Wk, L0_xattn_Wv, L0_xattn_Wo, L0_xattn_q_norm_w, L0_xattn_k_norm_w), axis=-1)
    x = _layernorm(x + _L0_ffn_ref(x, L0_ffn_w1q, L0_ffn_a1, L0_ffn_b1, L0_ffn_w3q, L0_ffn_a3, L0_ffn_b3, L0_ffn_w2q, L0_ffn_a2, L0_ffn_b2), axis=-1)
    return x

_drawn_inputs = setup_inputs


def setup_inputs(seed=0):
    import zlib

    import numpy as np

    out = dict(_drawn_inputs(seed))
    spreads = {'L0_xattn_q_norm_w': (1.0, 0.6), 'L0_xattn_k_norm_w': (1.0, 0.6)}
    factors = {'L0_ffn_a1': 8.0,
     'L0_ffn_b1': 8.0,
     'L0_ffn_a3': 8.0,
     'L0_ffn_b3': 8.0,
     'L0_ffn_a2': 8.0,
     'L0_ffn_b2': 8.0}
    for name, (base, spread) in spreads.items():
        noise = np.random.default_rng([zlib.crc32(name.encode()), seed]).standard_normal(out[name].shape)
        drawn = base * np.exp(spread * noise) if base else spread * noise
        out[name] = jnp.asarray(drawn.astype(out[name].dtype))
    for name, factor in factors.items():
        out[name] = (out[name] * factor).astype(out[name].dtype)
    return out
```

```python
from contextlib import ExitStack

import numpy as np

import concourse.bass as bass
from concourse import mybir

F32 = mybir.dt.float32
F32R = mybir.dt.float32r
ACT = mybir.ActivationFunctionType
ALU = mybir.AluOpType
AX = mybir.AxisListType

P = 128
B = 8
S = 128
D = 512
NC = D // P
HD = 128
G = 8
HPG = 4
STEPS = G * B
TOK = B * S
HALF = TOK // 2
SCALE = float(HD) ** -0.5
RMS_EPS = 1e-6
LN_EPS = 1e-5
FF = 1376
QF = FF // 4
KT = [128, 128, QF - 256]
NT = 4 * len(KT)
LORA = 0.5

B_S, B_T, B_O, B_Y, B_P0, B_P1 = 0, 2, 4, 5, 6, 7


def f32(ap):
    return ap.bitcast(F32)


def need(eng, sem, count):
    if isinstance(count, int) and count <= 0:
        return
    eng.wait_ge(sem, count)


def live(g, b, shift):
    return not isinstance(g, int) or 0 <= B * g + b + shift < STEPS


def build(nc, t):
    with ExitStack() as top:
        def alloc(scope, name, shape, dt=F32):
            return scope.enter_context(nc.sbuf_tensor(name, shape, dt))

        def sem(name):
            return top.enter_context(nc.semaphore(name))

        acc = alloc(top, "acc", [P, B, D])
        ident = alloc(top, "ident", [P, P])
        ones = alloc(top, "ones", [P, 1])
        mhalf = alloc(top, "mhalf", [P, 4])
        eps = alloc(top, "eps", [P, 2])
        bn6 = alloc(top, "bn6", [P, B, 6])
        mv = alloc(top, "mv", [P, B, 2])
        ve = alloc(top, "ve", [P, B])
        rstd = alloc(top, "rstd", [P, B])
        qw = alloc(top, "qw", [P, 1])
        kw = alloc(top, "kw", [P, 1])
        qkw = alloc(top, "qkw", [P, 1])
        ps = top.enter_context(nc.psum_tensor("ps", [P, 8, 512], F32))

        attn = ExitStack()
        xH = alloc(attn, "xH", [P, NC, TOK], F32R)
        xL = alloc(attn, "xL", [P, NC, TOK], F32R)
        cH = alloc(attn, "cH", [P, NC, TOK], F32R)
        cL = alloc(attn, "cL", [P, NC, TOK], F32R)
        QH = alloc(attn, "QH", [P, 2, HPG, HALF], F32R)
        QL = alloc(attn, "QL", [P, 2, HPG, HALF], F32R)
        KHL = alloc(attn, "KHL", [P, 2, 2, 2 * S], F32R)
        VH = alloc(attn, "VH", [P, 4, 2, HD], F32R)
        VL = alloc(attn, "VL", [P, 4, 2, HD], F32R)
        wqH = alloc(attn, "wqH", [P, HPG, NC, HD], F32R)
        wqL = alloc(attn, "wqL", [P, HPG, NC, HD], F32R)
        wkH = alloc(attn, "wkH", [P, NC, 2 * HD], F32R)
        wkL = alloc(attn, "wkL", [P, NC, 2 * HD], F32R)
        woH = alloc(attn, "woH", [P, HPG, D], F32R)
        woL = alloc(attn, "woL", [P, HPG, D], F32R)
        rawq = alloc(attn, "rawq", [P, 2, NC, HD])
        rawko = alloc(attn, "rawko", [P, HPG * D])
        pr = alloc(attn, "pr", [P, HPG, 2 * S])
        PH = alloc(attn, "PH", [P, 2, HPG * S], F32R)
        PL = alloc(attn, "PL", [P, 2, HPG * S], F32R)
        OH = alloc(attn, "OH", [P, 2, HPG * S], F32R)
        OL = alloc(attn, "OL", [P, 2, HPG * S], F32R)
        kraw = alloc(attn, "kraw", [P, 2, 2, HD])
        nmax = alloc(attn, "nmax", [P, HPG])
        nbias = alloc(attn, "nbias", [P, HPG])
        sums = alloc(attn, "sums", [P, HPG])
        rsum = alloc(attn, "rsum", [P, HPG])
        xraw = acc.rearrange("p b d -> p (b d)").rearrange("p (c n) -> p c n", c=NC)
        only1 = ExitStack()
        sc_b = alloc(only1, "sc_b", [P, HPG * S])
        bias = alloc(only1, "bias", [P, HPG * S])
        rawc = alloc(only1, "rawc", [P, 2, HALF])
        only1.close()
        only2 = ExitStack()
        kn = alloc(only2, "kn", [P, 2, HD])
        sq = alloc(only2, "sq", [P, HALF])
        junk = alloc(only2, "junk", [P, 2, HD])
        kss = alloc(only2, "kss", [P, 2, 2])
        kms = alloc(only2, "kms", [P, 2])
        krs = alloc(only2, "krs", [P, 2])
        qms = alloc(only2, "qms", [P, HPG])
        qsc = alloc(only2, "qsc", [P, 2, HPG, HPG])
        only2.close()
        attn.close()

        x2T = alloc(top, "x2T", [P, NC, TOK])
        xs = alloc(top, "xs", [P, B, P])
        xsH = alloc(top, "xsH", [P, TOK], F32R)
        xsL = alloc(top, "xsL", [P, TOK], F32R)
        wraw = alloc(top, "wraw", [P, 2, NT * P])
        wgH = alloc(top, "wgH", [P, 2, NT * P], F32R)
        wgL = alloc(top, "wgL", [P, 2, NT * P], F32R)
        braw = alloc(top, "braw", [P, 2, NT * P])
        bb = alloc(top, "bb", [P, 2, NT * P], F32R)
        apad = alloc(top, "apad", [P, NC, P])
        w2raw = alloc(top, "w2raw", [P, 3, D])
        w2H = alloc(top, "w2H", [P, 3, D], F32R)
        w2L = alloc(top, "w2L", [P, 3, D], F32R)
        a2pad = alloc(top, "a2pad", [P, NT, P])
        b2raw = alloc(top, "b2raw", [P, D])
        bb2 = alloc(top, "bb2", [P, D], F32R)
        tt = alloc(top, "tt", [P, TOK], F32R)
        tt2 = alloc(top, "tt2", [P, TOK], F32R)
        gate = alloc(top, "gate", [P, 2, HALF])
        mid = alloc(top, "mid", [P, 3, HALF])
        hs = alloc(top, "hs", [P, 3, HALF])
        hsH = alloc(top, "hsH", [P, 3, TOK], F32R)
        hsL = alloc(top, "hsL", [P, 3, TOK], F32R)

        def pair(name):
            return [sem(f"{name}{a}") for a in range(2)]
        q_done, kv_done, kt_done, sc_done = pair("q_done"), pair("kv_done"), pair("kt_done"), pair("sc_done")
        pt_done, pv_done, o_done = pair("pt_done"), pair("pv_done"), pair("o_done")
        sq_done = sem("sq_done")
        act_kv, act_k, act_p, act_exp, act_q, act_o = (pair(n) for n in (
            "act_kv", "act_k", "act_p", "act_exp", "act_q", "act_o"))
        dve_v, dve_k, dve_max, dve_p, dve_rs, dve_q, dve_o, dve_y = (pair(n) for n in (
            "dve_v", "dve_k", "dve_max", "dve_p", "dve_rs", "dve_q", "dve_o", "dve_y"))
        dve_bias, dve_add, dve_nm, dve_qms = sem("dve_bias"), sem("dve_add"), sem("dve_nm"), sem("dve_qms")
        pool_p = pair("pool_p")
        pool_kms, pool_krs, pool_k, pool_q = sem("pool_kms"), sem("pool_krs"), sem("pool_k"), sem("pool_q")
        in_q = [sem(f"in_q{i}") for i in range(2)]
        in_kv, in_o, in_bias = sem("in_kv"), sem("in_o"), sem("in_bias")
        in_x = [sem(f"in_x{i}") for i in range(2 * NC)]
        in_acc, in_w = sem("in_acc"), sem("in_w")
        in_c = [sem(f"in_c{i}") for i in range(2)]
        act_wq, act_wkv, act_wo = sem("act_wq"), sem("act_wkv"), sem("act_wo")
        pool_wq, pool_wo, dve_wkv, dve_wo = sem("pool_wq"), sem("pool_wo"), sem("dve_wkv"), sem("dve_wo")
        act_x, dve_x, act_c, pool_c = sem("act_x"), sem("dve_x"), sem("act_c"), sem("pool_c")
        z_id, id_ok, half_ok, ones_ok, qkw_ok = sem("z_id"), sem("id_ok"), sem("half_ok"), sem("ones_ok"), sem("qkw_ok")
        ln_bn, ln_mv, ln_ve, ln_rs, ln_ok = pair("ln_bn"), pair("ln_mv"), pair("ln_ve"), pair("ln_rs"), pair("ln_ok")
        lnt_done, act_lnt, dve_lnt = sem("lnt_done"), sem("act_lnt"), sem("dve_lnt")

        in_ff = [sem(f"in_ff{i}") for i in range(7)]
        zero_b = sem("zero_b")
        ff_xs, ff_t_done, ff_x2T, ff_xsH, ff_xsL = sem("ff_xs"), sem("ff_t_done"), sem("ff_x2T"), sem("ff_xsH"), sem("ff_xsL")
        ff_wH, ff_wL, ff_w2H, ff_w2L = sem("ff_wH"), sem("ff_wL"), sem("ff_w2H"), sem("ff_w2L")
        ff_bH, ff_bL, ff_b2H, ff_b2L = sem("ff_bH"), sem("ff_bL"), sem("ff_b2H"), sem("ff_b2L")
        lora_done, ff_ttH, ff_ttL = sem("lora_done"), sem("ff_ttH"), sem("ff_ttL")
        up_done, ff_gate, ff_mid, ff_hs = sem("up_done"), sem("ff_gate"), sem("ff_mid"), sem("ff_hs")
        lora2_done, ff_tt2H, ff_tt2L = sem("lora2_done"), sem("ff_tt2H"), sem("ff_tt2L")
        ff_hsH, ff_hsL, down_done, ff_y = sem("ff_hsH"), sem("ff_hsL"), sem("down_done"), sem("ff_y")
        l3_bn, l3_mv, l3_ve, l3_rs, l3_ok, out_ok = (sem(n) for n in ("l3_bn", "l3_mv", "l3_ve", "l3_rs", "l3_ok", "out_ok"))

        def steps(eng, a, step, last):
            for s in range(-4, B):
                step(a, s // B, s % B)
            with eng.Fori(1, G - 1) as g:
                for b in range(B):
                    step(a, g, b)
            for s in range(STEPS - B, last):
                step(a, s // B, s % B)

        def q_block(g, b):
            return g + (b + 4) // B, (b + 4) // 4 % 2, b % 4

        block = top.enter_context(nc.Block())

        @block.sync
        def _(sp):
            def load_q(w, m, first=False):
                if not first:
                    need(sp, pool_wq, HPG * w + m - 1)
                sp.dma_start(rawq[:, m % 2], t["wq"][w, m]).then_inc(in_q[m % 2], 16)

            def load_kv(w):
                need(sp, dve_wo, 2 * w)
                need(sp, pool_wo, 2 * w)
                sp.dma_start(rawko[:, 0:NC * 2 * HD], t["wkv"][w]).then_inc(in_kv, 16)

            def load_o(w):
                need(sp, dve_wkv, w + 1)
                sp.dma_start(rawko[:, :], t["wo"][w]).then_inc(in_o, 16)

            def load_bias(g):
                need(sp, dve_add, B * g)
                sp.dma_start(bias[:, :], t["bias"][g]).then_inc(in_bias, 16)

            load_q(0, 0, True)
            for i in range(2 * NC):
                n, c = i // NC, i % NC
                cols = slice(n * HALF, (n + 1) * HALF)
                sp.dma_start(xraw[:, c, cols], t["xT"][c][:, cols]).then_inc(in_x[i], 16)
                if i == NC - 1:
                    load_q(0, 1, True)
                    load_kv(0)
            load_q(0, 2)
            load_q(0, 3)
            load_bias(0)
            sp.wait_ge(dve_x, 2 * NC)
            sp.dma_start(acc[:, :, :], t["x"]).then_inc(in_acc, 16)
            sp.dma_start(qw[:, :], t["qw"]).then_inc(in_w, 16)
            sp.dma_start(kw[:, :], t["kw"]).then_inc(in_w, 16)

            def group(a, w, g, more):
                load_o(w)
                if more:
                    load_q(w + 1, 0)
                    load_q(w + 1, 1)
                    load_q(w + 1, 2)
                    load_q(w + 1, 3)
                    load_kv(w + 1)

            group(0, 0, 0, True)
            load_bias(1)
            with sp.Fori(1, G - 1) as g:
                group(0, g, g, True)
                load_bias(g + 1)
            def load_context(j):
                need(sp, pool_c, j - 1)
                sp.dma_start(rawc[:, j % 2], t["cT"][j // 2][:, (j % 2) * HALF:(j % 2 + 1) * HALF]).then_inc(in_c[j % 2], 16)
            load_context(0)
            load_context(1)
            group(0, G - 1, G - 1, True)
            for j in range(2, 2 * NC):
                load_context(j)
            with sp.Fori(G, 2 * G - 1) as w:
                group(1, w, w, True)
            group(1, 2 * G - 1, G - 1, False)

            need(sp, o_done[1], STEPS)
            need(sp, dve_y[1], STEPS)
            need(sp, zero_b, 1)
            for i in range(2):
                sp.dma_start(wraw[:, i], t["w13"][i]).then_inc(in_ff[i], 16)
            sp.dma_start(apad[:, :, :], t["apad"]).then_inc(in_ff[2], 16)
            for q in range(4):
                for i in range(2):
                    sp.dma_start(braw[32 * q + 2 * i:32 * q + 2 * i + 2, i, :], t["b13"][i]).then_inc(in_ff[3], 16)
                sp.dma_start(b2raw[32 * q:32 * q + 2, :], t["b2T"]).then_inc(in_ff[4], 16)
            sp.dma_start(a2pad[:, :, :], t["a2pad"]).then_inc(in_ff[5], 16)
            for k in range(3):
                sp.dma_start(w2raw[0:KT[k], k, :], t["w2T"][128 * k:128 * k + KT[k], :]).then_inc(in_ff[6], 16)
            for b in range(B):
                need(sp, l3_ok, b + 1)
                sp.dma_start(t["out"][b], acc[:, b, :]).then_inc(out_ok, 16)
            sp.wait_ge(out_ok, 16 * B)

        @block.tensor
        def _(pe):
            def parts(lH, lL, rH, rL):
                return ((lH, rH), (lH, rL), (lL, rH))

            def project_q(a, g, b):
                gq, half, m = q_block(g, b)
                n = B * g + b + 4
                s = B * g + b
                if half == 0:
                    need(pe, pool_wq, HPG * (gq + G * a) + m + 1)
                need(pe, dve_k[a], s + 1)
                if isinstance(g, int) and s < 0:
                    need(pe, dve_q[a], n)
                if a == 0 and isinstance(g, int) and n in (0, 4):
                    pe.wait_ge(dve_x, NC * (1 + half))
                if a == 1 and isinstance(g, int) and n in (0, 4):
                    need(pe, dve_lnt, B)
                for c in range(NC):
                    for i, (l, r) in enumerate(parts(wqH[:, m, c], wqL[:, m, c], xH[:, c, half * HALF:(half + 1) * HALF],
                                                     xL[:, c, half * HALF:(half + 1) * HALF])):
                        mm = pe.matmul(ps[:, B_P0, :], l, r, start=c == 0 and i == 0, stop=c == NC - 1 and i == 2)
                mm.then_inc(q_done[a], 1)

            def square_sums(n):
                need(pe, act_q[1], n + 1)
                need(pe, dve_qms, n)
                for i in range(HPG):
                    mm = pe.matmul(ps[:, B_T, i:i + 1], sq[:, i * S:(i + 1) * S], ones[:, :], start=i == 0,
                                   stop=i == HPG - 1, skip_group_check=True)
                mm.then_inc(sq_done, 1)

            def project_kv(a, g, b):
                s2 = B * g + b + 2
                bb_ = (b + 2) % B
                if bb_ == 0:
                    need(pe, dve_wkv, g + (b + 2) // B + G * a + 1)
                need(pe, dve_v[a], s2)
                if a == 0 and isinstance(g, int) and s2 == 0:
                    pe.wait_ge(dve_x, NC)
                if a == 1 and isinstance(g, int) and s2 == 0:
                    need(pe, pool_c, 2 * NC)
                    need(pe, dve_lnt, B)
                tiles = ((xH, xL),) if a == 0 else ((cH, cL), (xH, xL))
                for j, (sH, sL) in enumerate(tiles):
                    for c in range(NC):
                        tok = slice(bb_ * S, (bb_ + 1) * S)
                        for i, (l, r) in enumerate(parts(sH[:, c, tok], sL[:, c, tok], wkH[:, c, :], wkL[:, c, :])):
                            mm = pe.matmul(ps[:, B_P1, j * 2 * HD:(j + 1) * 2 * HD], l, r,
                                           start=c == 0 and i == 0, stop=c == NC - 1 and i == 2)
                mm.then_inc(kv_done[a], 1)

            def turn_keys(a, g, b):
                s1 = B * g + b + 1
                par = (b + 1) % 2
                if a == 0:
                    need(pe, act_kv[0], s1 + 1)
                else:
                    need(pe, pool_k, s1 + 1)
                need(pe, dve_q[a], B * g + b + 5 if live(g, b, 4) else STEPS)
                for j in range(a + 1):
                    src = kraw[:, par, 0] if a == 0 else kn[:, j]
                    mm = pe.transpose(ps[:, B_P0, j * S:(j + 1) * S], src, ident[:, :])
                mm.then_inc(kt_done[a], 1)

            def scores(a, g, b):
                s = B * g + b
                half, tok = b // 4, slice((b % 4) * S, (b % 4 + 1) * S)
                if b % 4 == 0:
                    need(pe, dve_q[a], s + 4)
                need(pe, dve_k[a], s + 1)
                need(pe, dve_add if a == 0 else act_exp[1], s)
                n = S * (a + 1)
                for h in range(HPG):
                    out = ps[:, B_S + h // 2, h % 2 * 256:h % 2 * 256 + 256]
                    if a == 0:
                        pe.matmul(out, QH[:, half, h, tok], KHL[:, b % 2, :, 0:n], start=True, stop=False,
                                  skip_group_check=True)
                        mm = pe.matmul(out[:, 0:n], QL[:, half, h, tok], KHL[:, b % 2, 0, 0:n], start=False, stop=True,
                                       skip_group_check=True)
                    else:
                        for i, (l, r) in enumerate(parts(QH[:, half, h, tok], QL[:, half, h, tok],
                                                         KHL[:, b % 2, 0], KHL[:, b % 2, 1])):
                            mm = pe.matmul(out, l, r, start=i == 0, stop=i == 2)
                mm.then_inc(sc_done[a], 1)

            def turn_probs(a, g, b):
                s = B * g + b
                need(pe, pool_p[a], s)
                if a == 1:
                    need(pe, dve_qms, s + 3 + 1 if live(g, b, 3) else STEPS)
                for j in range(a + 1):
                    for h in range(HPG):
                        mm = pe.transpose(ps[:, B_T + j, h * S:(h + 1) * S], pr[:, h, j * S:(j + 1) * S], ident[:, :])
                mm.then_inc(pt_done[a], 1)

            def weigh_values(a, g, b):
                s = B * g + b
                v = (b - 1) % 4
                need(pe, dve_p[a], s)
                need(pe, dve_v[a], s)
                need(pe, dve_o[a], s - 1)
                for j in range(a + 1):
                    for i, (l, r) in enumerate(parts(VH[:, v, j], VL[:, v, j], PH[:, j, :], PL[:, j, :])):
                        mm = pe.matmul(ps[:, B_O, :], l, r, start=j == 0 and i == 0, stop=j == a and i == 2)
                mm.then_inc(pv_done[a], 1)

            def project_out(a, g, b):
                s = B * g + b
                par = b % 2
                need(pe, dve_o[a], s - 1)
                need(pe, dve_y[a], s - 2)
                for h in range(HPG):
                    if b == 2:
                        need(pe, dve_wo if h < 2 else pool_wo, 2 * (g + G * a) + h % 2 + 1)
                    tok = slice(h * S, (h + 1) * S)
                    for i, (l, r) in enumerate(parts(OH[:, par, tok], OL[:, par, tok], woH[:, h], woL[:, h])):
                        mm = pe.matmul(ps[:, B_Y, :], l, r, start=h == 0 and i == 0, stop=h == HPG - 1 and i == 2)
                mm.then_inc(o_done[a], 1)

            def turn_norm(b):
                need(pe, ln_ok[0], b + 1)
                need(pe, dve_k[0], min(b + STEPS - 4 + 1, STEPS))
                need(pe, dve_q[0], STEPS)
                need(pe, dve_lnt, b)
                for c in range(NC):
                    mm = pe.transpose(ps[:, B_P0, c * P:(c + 1) * P], acc[:, b, c * P:(c + 1) * P], ident[:, :])
                mm.then_inc(lnt_done, 1)

            def step(a, g, b):
                if live(g, b, 0):
                    scores(a, g, b)
                if live(g, b, -1):
                    turn_probs(a, g, b)
                if live(g, b, 4):
                    project_q(a, g, b)
                if a == 0 and isinstance(g, int) and B * g + b >= STEPS - 4:
                    turn_norm(B * g + b - (STEPS - 4))
                last = isinstance(g, int) and B * g + b >= STEPS - 4
                if last and live(g, b, -2):
                    project_out(a, g, b)
                if live(g, b, -1):
                    weigh_values(a, g, b)
                if not last and live(g, b, -2):
                    project_out(a, g, b)
                if a == 1 and live(g, b, 4):
                    first = isinstance(g, int) and g < 0
                    if not first:
                        square_sums(B * g + b + 4)
                    elif b > 4:
                        square_sums(b - 5)
                if live(g, b, 1):
                    if a == 0 and isinstance(g, int) and STEPS - 4 <= B * g + b:
                        need(pe, dve_lnt, B * g + b - (STEPS - 4) + 1)
                    turn_keys(a, g, b)
                if live(g, b, 2):
                    project_kv(a, g, b)
                if a == 1 and isinstance(g, int) and (g, b) == (-1, B - 1):
                    square_sums(3)

            pe.wait_ge(id_ok, 1)
            pe.wait_ge(ones_ok, 1)
            steps(pe, 0, step, STEPS + 4)
            steps(pe, 1, step, STEPS + 2)

            for b in range(B):
                need(pe, ln_ok[1], b + 1)
                need(pe, ff_xs, b + 1)
                need(pe, ff_x2T, 2 * (b - 1))
                need(pe, ff_xsL, b - 1)
                for c in range(NC):
                    pe.transpose(ps[:, b % 2, c * P:(c + 1) * P], acc[:, b, c * P:(c + 1) * P], ident[:, :])
                pe.transpose(ps[:, 2 + b % 2, 0:P], xs[:, b, :], ident[:, :]).then_inc(ff_t_done, 1)
            pe.wait_ge(in_ff[2], 16)
            for n in range(2):
                need(pe, ff_x2T, 8 + 8 * n)
                for c in range(NC):
                    mm = pe.matmul(ps[:, 4 + n, :], apad[:, c, :], x2T[:, c, n * HALF:(n + 1) * HALF],
                                   start=c == 0, stop=c == NC - 1)
                mm.then_inc(lora_done, 1)
            pe.wait_ge(in_ff[5], 16)
            pe.wait_ge(ff_wL, 2)
            pe.wait_ge(ff_bL, 2)
            pe.wait_ge(ff_xsL, B)

            def lora2(n, k):
                rows = KT[k % 3]
                need(pe, ff_mid, n * NT + k + 1)
                mm = pe.matmul(ps[:, 4 + n, :], a2pad[0:rows, k, :], mid[0:rows, (n * NT + k) % 3, :],
                               start=k == 0, stop=k == NT - 1)
                mm.then_inc(lora2_done, 1)

            for n in range(2):
                need(pe, ff_ttL, n + 1)
                for k in range(NT):
                    u = n * NT + k
                    rows = KT[k % 3]
                    cols = slice(k * P, k * P + rows)
                    tok = slice(n * HALF, (n + 1) * HALF)
                    need(pe, ff_mid, u - 1)
                    for i in range(2):
                        out = ps[0:rows, 2 * (u % 2) + i, :]
                        for j, (l, r) in enumerate(parts(wgH[:, i, cols], wgL[:, i, cols], xsH[:, tok], xsL[:, tok])):
                            pe.matmul(out, l, r, start=j == 0, stop=False)
                        mm = pe.matmul(out, bb[:, i, cols], tt[:, tok], start=False, stop=True)
                    mm.then_inc(up_done, 1)
                    if k >= 1:
                        lora2(n, k - 1)
                lora2(n, NT - 1)

            pe.wait_ge(ff_w2L, 1)
            pe.wait_ge(ff_b2L, 1)
            for b in range(B):
                tok = slice(b * S, (b + 1) * S)
                if b % 4 == 0:
                    need(pe, ff_hsL, 3 * (b // 4 + 1))
                    need(pe, ff_tt2L, b // 4 + 1)
                need(pe, ff_y, b - 1)
                for k in range(3):
                    rows = KT[k]
                    for i, (l, r) in enumerate(parts(hsH[0:rows, k, tok], hsL[0:rows, k, tok],
                                                     w2H[0:rows, k], w2L[0:rows, k])):
                        pe.matmul(ps[:, 6 + b % 2, :], l, r, start=k == 0 and i == 0, stop=False)
                pe.matmul(ps[:, 6 + b % 2, :], tt2[:, tok], bb2[:, :], start=False, stop=True).then_inc(down_done, 1)

        @block.scalar
        def _(act):
            def high(out, src, scale=1.0):
                return act.activation(out, src, ACT.Copy, scale=scale)

            def split_wq(w, m):
                need(act, in_q[m % 2], 16 * (2 * w + m // 2 + 1))
                high(wqH[:, m], rawq[:, m % 2]).then_inc(act_wq, 1)

            def split_wkv(w):
                need(act, in_kv, 16 * (w + 1))
                high(wkH[:, :, :], rawko[:, 0:NC * 2 * HD].rearrange("p (c n) -> p c n", c=NC)).then_inc(act_wkv, 1)

            def split_wo(w):
                need(act, in_o, 16 * (w + 1))
                for h in range(HPG):
                    high(woH[:, h], rawko[:, h * D:(h + 1) * D]).then_inc(act_wo, 1)

            def step(a, g, b):
                s = B * g + b
                w = g + G * a
                if live(g, b, 1):
                    need(act, kv_done[a], s + 2)
                    kv = ps[:, B_P1, 0:(a + 1) * 2 * HD].rearrange("p (j n) -> p j n", n=2 * HD)
                    v, par = (b + 1) % 4, (b + 1) % 2
                    high(VH[:, v, 0:a + 1], kv[:, :, HD:2 * HD])
                    if a == 0:
                        act.activation(kraw[:, par, 0:1], kv[:, :, 0:HD], ACT.Copy).then_inc(act_kv[0], 1)
                    else:
                        act.activation(kraw[:, par, 0:2], kv[:, :, 0:HD], ACT.Copy)
                        for j in range(2):
                            x = act.activation(junk[:, j], kv[:, j, 0:HD], ACT.Square, scale=SCALE, accum_out=kss[:, par, j:j + 1])
                        x.then_inc(act_kv[1], 1)
                if live(g, b, -1):
                    need(act, pt_done[a], s)
                    for j in range(a + 1):
                        x = high(PH[:, j], ps[:, B_T + j, :])
                    x.then_inc(act_p[a], 1)
                if b == 2 and live(g, b, -2):
                    need(act, o_done[a], s - 2)
                    if a == 1 and isinstance(g, int) and g == 0:
                        need(act, o_done[0], STEPS)
                    split_wo(w)
                if live(g, b, 0):
                    need(act, dve_max[a], s + 1)
                    half = b // 4
                    for h in range(HPG):
                        if a == 0:
                            x = act.activation(pr[:, h, 0:S], sc_b[:, h * S:(h + 1) * S], ACT.Exp,
                                               bias=nmax[:, h:h + 1], accum_out=sums[:, h:h + 1])
                        else:
                            x = act.activation(pr[:, h, :], ps[:, B_S + h // 2, (h % 2) * 256:(h % 2 + 1) * 256], ACT.Exp,
                                               bias=nbias[:, h:h + 1], scale=qsc[:, half, h, b % 4:b % 4 + 1],
                                               accum_out=sums[:, h:h + 1])
                    x.then_inc(act_exp[a], 1)
                if live(g, b, 4):
                    _, half, m = q_block(g, b)
                    need(act, q_done[a], s + 5)
                    x = high(QH[:, half, m], ps[:, B_P0, :], SCALE if a == 0 else 1.0)
                    if a == 1:
                        need(act, sq_done, s + 4)
                        x = act.activation(sq[:, :], ps[:, B_P0, :], ACT.Square)
                    x.then_inc(act_q[a], 1)
                if a == 0 and isinstance(g, int) and s >= STEPS - 4:
                    c = s - (STEPS - 4)
                    need(act, lnt_done, c + 1)
                    high(xH[:, :, c * S:(c + 1) * S], ps[:, B_P0, :].rearrange("p (c n) -> p c n", c=NC)).then_inc(act_lnt, 1)
                if live(g, b, -1):
                    need(act, pv_done[a], s)
                    need(act, o_done[a], s - 2)
                    high(OH[:, (b - 1) % 2], ps[:, B_O, :]).then_inc(act_o[a], 1)
                refill = not isinstance(g, int) or (0 <= g < G and w + 1 < 2 * G)
                if b < 4 and refill:
                    split_wq(w + 1, b)
                if b == 6 and refill:
                    need(act, kv_done[a], s + 2)
                    split_wkv(w + 1)
                if live(g, b, 1):
                    need(act, kt_done[a], s + 2)
                    n, par = S * (a + 1), (b + 1) % 2
                    high(KHL[:, par, 0, 0:n], ps[:, B_P0, 0:n], 1.0 if a == 0 else qkw[:, 0:1]).then_inc(act_k[a], 1)
                if a == 0 and isinstance(g, int) and g == G - 1:
                    need(act, in_c[b % 2], 16 * (b // 2 + 1))
                    high(cH[:, b // 2, (b % 2) * HALF:(b % 2 + 1) * HALF], rawc[:, b % 2]).then_inc(act_c, 1)

            split_wq(0, 0)
            def split_x(n):
                for c in range(NC):
                    cols = slice(n * HALF, (n + 1) * HALF)
                    act.wait_ge(in_x[n * NC + c], 16)
                    high(xH[:, c, cols], xraw[:, c, cols]).then_inc(act_x, 1)

            split_x(0)
            split_wq(0, 1)
            split_wkv(0)
            split_x(1)
            split_wq(0, 2)
            split_wq(0, 3)
            steps(act, 0, step, STEPS + 4)
            act.wait_ge(qkw_ok, 1)
            steps(act, 1, step, STEPS + 2)

            for i in range(2):
                act.wait_ge(in_ff[i], 16)
                high(wgH[:, i], wraw[:, i]).then_inc(ff_wH, 1)
            for b in range(B):
                need(act, ff_t_done, b + 1)
                act.activation(x2T[:, :, b * S:(b + 1) * S], ps[:, b % 2, :].rearrange("p (c n) -> p c n", c=NC),
                               ACT.Copy).then_inc(ff_x2T, 2)
                high(xsH[:, b * S:(b + 1) * S], ps[:, 2 + b % 2, 0:P]).then_inc(ff_xsH, 1)
                if b == 2:
                    act.wait_ge(in_ff[3], 16 * 8)
                    for i in range(2):
                        high(bb[:, i], braw[:, i]).then_inc(ff_bH, 1)
            for n in range(2):
                need(act, lora_done, n + 1)
                high(tt[:, n * HALF:(n + 1) * HALF], ps[:, 4 + n, :], LORA).then_inc(ff_ttH, 1)
            for n in range(2):
                for k in range(NT):
                    u = n * NT + k
                    rows = KT[k % 3]
                    need(act, up_done, u + 1)
                    need(act, ff_mid, u - 1)
                    act.activation(gate[0:rows, u % 2], ps[0:rows, 2 * (u % 2), :], ACT.Silu).then_inc(ff_gate, 1)
                need(act, lora2_done, NT * (n + 1))
                high(tt2[:, n * HALF:(n + 1) * HALF], ps[:, 4 + n, :], LORA).then_inc(ff_tt2H, 1)
                for k in range(3):
                    need(act, ff_hs, n * NT + 9 + k + 1)
                    high(hsH[0:KT[k], k, n * HALF:(n + 1) * HALF], hs[0:KT[k], k, :]).then_inc(ff_hsH, 1)
                if n == 0:
                    act.wait_ge(in_ff[6], 16 * 3)
                    for k in range(3):
                        x = high(w2H[0:KT[k], k], w2raw[0:KT[k], k])
                    x.then_inc(ff_w2H, 1)
                    act.wait_ge(in_ff[4], 16 * 4)
                    high(bb2[:, :], b2raw[:, :]).then_inc(ff_b2H, 1)

        @block.vector
        def _(dve):
            def low(out, src, hi):
                return dve.tensor_tensor(out, src, f32(hi), ALU.subtract)

            def split_wkv(w):
                need(dve, act_wkv, w + 1)
                low(wkL[:, :, :], rawko[:, 0:NC * 2 * HD].rearrange("p (c n) -> p c n", c=NC), wkH[:, :, :]).then_inc(dve_wkv, 1)

            def norm_stats(a, b):
                dve.bn_stats(bn6[:, b, :], acc[:, b, :]).then_inc(ln_bn[a], 1)
                need(dve, ln_bn[a], b + 1)
                dve.bn_aggr(mv[:, b, :], bn6[:, b, :]).then_inc(ln_mv[a], 1)
                need(dve, ln_mv[a], b + 1)
                dve.tensor_scalar(ve[:, b:b + 1], mv[:, b, 1:2], LN_EPS, None, ALU.add).then_inc(ln_ve[a], 1)

            def norm_apply(a, b):
                need(dve, ln_rs[a], b + 1)
                dve.tensor_scalar(acc[:, b, :], acc[:, b, :], mv[:, b, 0:1], rstd[:, b:b + 1],
                                  ALU.subtract, ALU.mult).then_inc(ln_ok[a], 1)

            def step(a, g, b):
                s = B * g + b
                w = g + G * a
                if live(g, b, 1):
                    need(dve, act_kv[a], s + 2)
                    kv = ps[:, B_P1, 0:(a + 1) * 2 * HD].rearrange("p (j n) -> p j n", n=2 * HD)
                    v = (b + 1) % 4
                    low(VL[:, v, 0:a + 1], kv[:, :, HD:2 * HD], VH[:, v, 0:a + 1]).then_inc(dve_v[a], 1)
                if live(g, b, 0):
                    need(dve, sc_done[a], s + 1)
                    if a == 0:
                        if b == 0:
                            need(dve, in_bias, 16 * (g + 1))
                        need(dve, act_exp[0], s)
                        both = ps[:, B_S:B_S + 2, :].rearrange("p j (h i k) -> p (j h) i k", h=2, i=2)
                        shaped = [v[:, :].rearrange("p (h k) -> p h k", h=HPG) for v in (sc_b, bias)]
                        dve.tensor_tensor(shaped[0], both[:, :, 1], shaped[1], ALU.add).then_inc(dve_bias, 1)
                        need(dve, dve_bias, s + 1)
                        dve.tensor_tensor(shaped[0], both[:, :, 0], shaped[0], ALU.add).then_inc(dve_add, 1)
                        need(dve, dve_add, s + 1)
                        dve.tensor_reduce(nmax[:, :], sc_b[:, :].rearrange("p (h k) -> p h k", h=HPG), AX.X, ALU.max,
                                          negate=True).then_inc(dve_max[0], 1)
                    else:
                        dve.tensor_reduce(nmax[:, :], ps[:, B_S:B_S + 2, :].rearrange("p j (h k) -> p (j h) k", h=2),
                                          AX.X, ALU.max, negate=True).then_inc(dve_nm, 1)
                        need(dve, dve_nm, s + 1)
                        if b % 4 == 0:
                            need(dve, pool_q, s + 4)
                        need(dve, act_exp[1], s)
                        dve.tensor_tensor(nbias[:, :], nmax[:, :], qsc[:, b // 4, :, b % 4], ALU.mult).then_inc(dve_max[1], 1)
                if live(g, b, -1):
                    need(dve, act_p[a], s)
                    for j in range(a + 1):
                        x = low(PL[:, j], ps[:, B_T + j, :], PH[:, j])
                    x.then_inc(dve_p[a], 1)
                if isinstance(g, int) and s - 3 >= STEPS - B and live(g, b, -3):
                    norm_apply(a, s - 3 - (STEPS - B))
                if b == 2 and live(g, b, -2):
                    for h in range(2):
                        need(dve, act_wo, HPG * w + h + 1)
                        low(woL[:, h], rawko[:, h * D:(h + 1) * D], woH[:, h]).then_inc(dve_wo, 1)
                if live(g, b, 0):
                    need(dve, act_exp[a], s + 1)
                    need(dve, pool_p[a], s)
                    dve.reciprocal(rsum[:, :], sums[:, :]).then_inc(dve_rs[a], 1)
                if live(g, b, 4):
                    _, half, m = q_block(g, b)
                    need(dve, act_q[a], s + 5)
                    if a == 0:
                        dve.scalar_tensor_tensor(out=QL[:, half, m], in0=ps[:, B_P0, :], scalar=SCALE, in1=f32(QH[:, half, m]),
                                                 op0=ALU.mult, op1=ALU.subtract).then_inc(dve_q[0], 1)
                    else:
                        low(QL[:, half, m], ps[:, B_P0, :], QH[:, half, m]).then_inc(dve_q[1], 1)
                if a == 0 and isinstance(g, int) and s >= STEPS - 4:
                    c = s - (STEPS - 4)
                    need(dve, act_lnt, c + 1)
                    low(xL[:, :, c * S:(c + 1) * S], ps[:, B_P0, :].rearrange("p (c n) -> p c n", c=NC),
                        xH[:, :, c * S:(c + 1) * S]).then_inc(dve_lnt, 1)
                if live(g, b, -1):
                    need(dve, act_o[a], s)
                    low(OL[:, (b - 1) % 2], ps[:, B_O, :], OH[:, (b - 1) % 2]).then_inc(dve_o[a], 1)
                refill = not isinstance(g, int) or (0 <= g < G and w + 1 < 2 * G)
                if b == 6 and refill:
                    split_wkv(w + 1)
                if live(g, b, -2):
                    bb_ = (b - 2) % B
                    need(dve, o_done[a], s - 1)
                    need(dve, dve_y[a], s - 2)
                    dve.tensor_tensor(acc[:, bb_, :], ps[:, B_Y, :], acc[:, bb_, :], ALU.add).then_inc(dve_y[a], 1)
                if isinstance(g, int) and s - 2 >= STEPS - B and live(g, b, -2):
                    need(dve, dve_y[a], s - 1)
                    norm_stats(a, s - 2 - (STEPS - B))
                if a == 1 and live(g, b, 4):
                    need(dve, sq_done, s + 5)
                    need(dve, pool_q, s + 4)
                    dve.tensor_scalar(qms[:, :], ps[:, B_T, 0:HPG], HD * RMS_EPS, None, ALU.add).then_inc(dve_qms, 1)
                if live(g, b, 1):
                    need(dve, act_k[a], s + 2)
                    n, par = S * (a + 1), (b + 1) % 2
                    if a == 0:
                        low(KHL[:, par, 1, 0:n], ps[:, B_P0, 0:n], KHL[:, par, 0, 0:n]).then_inc(dve_k[0], 1)
                    else:
                        dve.scalar_tensor_tensor(out=KHL[:, par, 1, 0:n], in0=ps[:, B_P0, 0:n], scalar=qkw[:, 0:1],
                                                 in1=f32(KHL[:, par, 0, 0:n]), op0=ALU.mult, op1=ALU.subtract).then_inc(dve_k[1], 1)

            def split_x(n):
                for c in range(NC):
                    cols = slice(n * HALF, (n + 1) * HALF)
                    need(dve, act_x, n * NC + c + 1)
                    low(xL[:, c, cols], xraw[:, c, cols], xH[:, c, cols]).then_inc(dve_x, 1)

            split_x(0)
            split_wkv(0)
            split_x(1)
            dve.wait_ge(in_acc, 16)
            steps(dve, 0, step, STEPS + 4)
            dve.wait_ge(in_w, 32)
            dve.tensor_tensor(qkw[:, :], qw[:, :], kw[:, :], ALU.mult).then_inc(qkw_ok, 1)
            dve.wait_ge(qkw_ok, 1)
            steps(dve, 1, step, STEPS + 3)

            for b in range(B):
                need(dve, ln_ok[1], b + 1)
                dve.tensor_reduce(xs[:, b, :], acc[:, b, :].rearrange("p (c f) -> p f c", c=NC), AX.X, ALU.add).then_inc(ff_xs, 1)
            for i in range(2):
                need(dve, ff_wH, i + 1)
                low(wgL[:, i], wraw[:, i], wgH[:, i]).then_inc(ff_wL, 1)
            for b in range(B):
                need(dve, ff_xsH, b + 1)
                low(xsL[:, b * S:(b + 1) * S], ps[:, 2 + b % 2, 0:P], xsH[:, b * S:(b + 1) * S]).then_inc(ff_xsL, 1)
            for i in range(2):
                need(dve, ff_bH, i + 1)
                for q in (1, 3):
                    r = slice(32 * q, 32 * q + 32)
                    x = low(bb[r, i], braw[r, i], bb[r, i])
                x.then_inc(ff_bL, 1)
            for n in range(2):
                need(dve, ff_ttH, n + 1)
                cols = slice(n * HALF, (n + 1) * HALF)
                dve.scalar_tensor_tensor(out=tt[64:128, cols], in0=ps[64:128, 4 + n, :], scalar=LORA, in1=f32(tt[64:128, cols]),
                                         op0=ALU.mult, op1=ALU.subtract).then_inc(ff_ttL, 1)
            for n in range(2):
                for k in range(NT):
                    u = n * NT + k
                    rows = KT[k % 3]
                    need(dve, ff_gate, u + 1)
                    need(dve, lora2_done, u - 2)
                    need(dve, ff_hs, u - 2)
                    dve.tensor_tensor(mid[0:rows, u % 3], ps[0:rows, 2 * (u % 2) + 1, :], gate[0:rows, u % 2],
                                      ALU.mult).then_inc(ff_mid, 1)
                for k in range(3):
                    need(dve, ff_hsH, n * 3 + k + 1)
                    cols = slice(n * HALF, (n + 1) * HALF)
                    low(hsL[0:KT[k], k, cols], hs[0:KT[k], k, :], hsH[0:KT[k], k, cols]).then_inc(ff_hsL, 1)
                need(dve, ff_tt2H, n + 1)
                dve.scalar_tensor_tensor(out=tt2[64:128, cols], in0=ps[64:128, 4 + n, :], scalar=LORA,
                                         in1=f32(tt2[64:128, cols]), op0=ALU.mult, op1=ALU.subtract).then_inc(ff_tt2L, 1)
                if n == 0:
                    need(dve, ff_w2H, 1)
                    for k in range(3):
                        x = low(w2L[0:KT[k], k], w2raw[0:KT[k], k], w2H[0:KT[k], k])
                    x.then_inc(ff_w2L, 1)
                    need(dve, ff_b2H, 1)
                    for q in (1, 3):
                        r = slice(32 * q, 32 * q + 32)
                        x = low(bb2[r, :], b2raw[r, :], bb2[r, :])
                    x.then_inc(ff_b2L, 1)
            for b in range(B + 1):
                if b < B:
                    need(dve, down_done, b + 1)
                    dve.tensor_tensor(acc[:, b, :], ps[:, 6 + b % 2, :], acc[:, b, :], ALU.add).then_inc(ff_y, 1)
                    need(dve, ff_y, b + 1)
                    dve.bn_stats(bn6[:, b, :], acc[:, b, :]).then_inc(l3_bn, 1)
                    need(dve, l3_bn, b + 1)
                    dve.bn_aggr(mv[:, b, :], bn6[:, b, :]).then_inc(l3_mv, 1)
                    need(dve, l3_mv, b + 1)
                    dve.tensor_scalar(ve[:, b:b + 1], mv[:, b, 1:2], LN_EPS, None, ALU.add).then_inc(l3_ve, 1)
                if b >= 1:
                    c = b - 1
                    need(dve, l3_rs, c + 1)
                    dve.tensor_scalar(acc[:, c, :], acc[:, c, :], mv[:, c, 0:1], rstd[:, c:c + 1],
                                      ALU.subtract, ALU.mult).then_inc(l3_ok, 1)

        @block.gpsimd
        def _(pool):
            def low(out, src, hi):
                return pool.tensor_tensor(out, src, f32(hi), ALU.subtract)

            def split_wq(w, m):
                need(pool, act_wq, HPG * w + m + 1)
                low(wqL[:, m], rawq[:, m % 2], wqH[:, m]).then_inc(pool_wq, 1)

            def step(a, g, b):
                s = B * g + b
                w = g + G * a
                if b == 2 and live(g, b, -2):
                    for h in range(2, HPG):
                        need(pool, act_wo, HPG * w + h + 1)
                        low(woL[:, h], rawko[:, h * D:(h + 1) * D], woH[:, h]).then_inc(pool_wo, 1)
                if a == 1 and live(g, b, 1):
                    par = (b + 1) % 2
                    need(pool, act_kv[1], s + 2)
                    pool.tensor_tensor(kms[:, :], kss[:, par, :], eps[:, :], ALU.add).then_inc(pool_kms, 1)
                    need(pool, pool_kms, s + 2)
                    pool.tensor_tensor(krs[:, :], kms[:, :], mhalf[:, 0:2], ALU.pow).then_inc(pool_krs, 1)
                    need(pool, pool_krs, s + 2)
                    need(pool, kt_done[1], s + 1)
                    pool.tensor_tensor(kn[:, :, :], kraw[:, par], krs[:, :].unsqueeze(2).to_broadcast([P, 2, HD]),
                                       ALU.mult).then_inc(pool_k, 1)
                if live(g, b, 0):
                    need(pool, dve_rs[a], s + 1)
                    n = S * (a + 1)
                    pool.tensor_tensor(pr[:, 0, 0:n], pr[:, 0, 0:n], rsum[:, 0:1].to_broadcast([P, n]), ALU.mult)
                    for h in range(1, HPG):
                        x = pool.tensor_scalar(pr[:, h, 0:n], pr[:, h, 0:n], rsum[:, h:h + 1], 1.0, ALU.mult, ALU.mult)
                    x.then_inc(pool_p[a], 1)
                refill = not isinstance(g, int) or (0 <= g < G and w + 1 < 2 * G)
                if b < 4 and refill:
                    split_wq(w + 1, b)
                if a == 0 and isinstance(g, int) and g == G - 1:
                    need(pool, act_c, b + 1)
                    cols = slice((b % 2) * HALF, (b % 2 + 1) * HALF)
                    low(cL[:, b // 2, cols], rawc[:, b % 2], cH[:, b // 2, cols]).then_inc(pool_c, 1)
                if a == 1 and live(g, b, 4):
                    _, half, m = q_block(g, b)
                    need(pool, dve_qms, s + 5)
                    pool.tensor_tensor(qsc[:, half, m, :], qms[:, :], mhalf[:, :], ALU.pow).then_inc(pool_q, 1)
                if isinstance(g, int) and s - 2 >= STEPS - B and live(g, b, -2):
                    c = s - 2 - (STEPS - B)
                    need(pool, ln_ve[a], c + 1)
                    pool.tensor_tensor(rstd[:, c:c + 1], ve[:, c:c + 1], mhalf[:, 0:1], ALU.pow).then_inc(ln_rs[a], 1)

            pool.memset(ident[:, :], 0.0).then_inc(z_id, 1)
            pool.wait_ge(z_id, 1)
            pool.affine_select(out=ident[:, :], in_=ident[:, :], compare_op=ALU.not_equal, fill=1.0, base=0,
                               pattern=[[-1, P]], channel_multiplier=1).then_inc(id_ok, 1)
            pool.memset(ones[:, :], 1.0).then_inc(ones_ok, 1)
            pool.memset(eps[:, :], RMS_EPS)
            pool.memset(mhalf[:, :], -0.5).then_inc(half_ok, 1)
            pool.wait_ge(half_ok, 1)
            for m in range(HPG):
                split_wq(0, m)
            steps(pool, 0, step, STEPS + 4)
            steps(pool, 1, step, STEPS + 2)

            pool.wait_ge(o_done[1], STEPS)
            pool.wait_ge(dve_y[1], STEPS)
            pool.memset(braw[:, :, :], 0.0)
            pool.memset(b2raw[:, :], 0.0).then_inc(zero_b, 1)
            for n in range(2):
                for k in range(NT):
                    u = n * NT + k
                    rows = KT[k % 3]
                    need(pool, ff_mid, u + 1)
                    src = mid[0:rows, u % 3]
                    out = hs[0:rows, k % 3]
                    if k < 3:
                        if n == 1:
                            need(pool, ff_hsL, k + 1)
                        pool.tensor_copy(out, src).then_inc(ff_hs, 1)
                    else:
                        need(pool, ff_hs, u - 2)
                        pool.tensor_tensor(out, out, src, ALU.add).then_inc(ff_hs, 1)
            for b in range(B):
                need(pool, l3_ve, b + 1)
                pool.tensor_tensor(rstd[:, b:b + 1], ve[:, b:b + 1], mhalf[:, 0:1], ALU.pow).then_inc(l3_rs, 1)



def kernel(x, ctx_4096, L0_attn_w_qkv, L0_attn_w_o, L0_xattn_Wq, L0_xattn_Wk, L0_xattn_Wv, L0_xattn_Wo,
           L0_xattn_q_norm_w, L0_xattn_k_norm_w, L0_ffn_w1q, L0_ffn_a1, L0_ffn_b1, L0_ffn_w3q, L0_ffn_a3, L0_ffn_b3,
           L0_ffn_w2q, L0_ffn_a2, L0_ffn_b2):
    import concourse.bacc as bacc
    from concourse.bass_utils import run_bass_kernel_spmd

    def arr(v):
        return np.asarray(v)

    def columns(w, n):
        return w.reshape(NC, P, n, HD).transpose(2, 1, 0, 3)

    w_qkv = arr(L0_attn_w_qkv)
    q1, k1, v1 = w_qkv[:, :G * HPG * HD], w_qkv[:, G * HPG * HD:G * (HPG + 1) * HD], w_qkv[:, G * (HPG + 1) * HD:]
    wq = np.stack([columns(q1, G * HPG), columns(arr(L0_xattn_Wq), G * HPG)]).reshape(2 * G, HPG, P, NC, HD)
    wkv = np.stack([np.concatenate([columns(k, G), columns(v, G)], axis=3)
                    for k, v in ((k1, v1), (arr(L0_xattn_Wk), arr(L0_xattn_Wv)))]).reshape(2 * G, P, NC * 2 * HD)
    wo = np.stack([arr(L0_attn_w_o), arr(L0_xattn_Wo)]).reshape(2 * G, HPG, HD, D).transpose(0, 2, 1, 3).reshape(2 * G, P, HPG * D)

    slope = ((2.0 ** (-8.0 / (G * HPG))) ** np.arange(1, G * HPG + 1, dtype=np.float32)).astype(np.float32)
    rel = np.arange(S)[:, None] - np.arange(S)[None, :]
    dist = np.sqrt(np.maximum(rel, 0).astype(np.float32))
    bias = np.where(rel[None] >= 0, -slope[:, None, None] * dist, np.float32(-1e30)).astype(np.float32)
    bias = bias.reshape(G, HPG, S, S).transpose(0, 2, 1, 3).reshape(G, S, HPG * S)

    def hidden_tiles(w):
        out = np.zeros(w.shape[:-1] + (NT, P), w.dtype)
        for k in range(NT):
            at = k // 3 * QF + k % 3 * P
            out[..., k, :KT[k % 3]] = w[..., at:at + KT[k % 3]]
        return out

    def copies(*factors):
        out = np.zeros((factors[0].shape[1], 4, 32), factors[0].dtype)
        for i, f in enumerate(factors):
            out[:, :, 2 * i:2 * i + 2] = f.T[:, None, :]
        return out.reshape(-1, P)

    w13 = np.stack([hidden_tiles(arr(w).T).reshape(P, NT * P) for w in (L0_ffn_w1q, L0_ffn_w3q)])
    b13 = np.stack([hidden_tiles(arr(w).T).reshape(2, NT * P) for w in (L0_ffn_b1, L0_ffn_b3)])
    apad = copies(arr(L0_ffn_a1), arr(L0_ffn_a3)).reshape(NC, P, P).transpose(1, 0, 2)
    a2pad = hidden_tiles(copies(arr(L0_ffn_a2)).T).transpose(2, 1, 0)
    data = {
        "xT": arr(x).reshape(TOK, D).T.reshape(NC, P, TOK), "x": arr(x).transpose(1, 0, 2),
        "cT": arr(ctx_4096).reshape(TOK, D).T.reshape(NC, P, TOK),
        "wq": wq, "wkv": wkv, "wo": wo, "bias": bias,
        "qw": arr(L0_xattn_q_norm_w).reshape(P, 1), "kw": arr(L0_xattn_k_norm_w).reshape(P, 1),
        "w13": w13, "b13": b13, "apad": apad, "a2pad": a2pad,
        "w2T": arr(L0_ffn_w2q).T, "b2T": arr(L0_ffn_b2).T,
    }
    data = {n: np.ascontiguousarray(v) for n, v in data.items()}
    nc = bacc.Bacc("TRN2", target_bir_lowering=False, num_devices=1)
    t = {n: nc.dram_tensor(f"in_{n}", v.shape, F32, kind="ExternalInput").ap() for n, v in data.items()}
    t["out"] = nc.dram_tensor("out", (B, S, D), F32, kind="ExternalOutput").ap()
    build(nc, t)
    r = run_bass_kernel_spmd(nc, [{f"in_{n}": v for n, v in data.items()}], core_ids=[0])
    return r.results[0]["out"]
```

```python
from contextlib import ExitStack

import numpy as np

import concourse.bass as bass
from concourse import mybir

F32 = mybir.dt.float32
F32R = mybir.dt.float32r
ACT = mybir.ActivationFunctionType
ALU = mybir.AluOpType
AX = mybir.AxisListType

P = 128
B = 8
S = 128
D = 512
NC = D // P
HD = 128
G = 8
HPG = 4
STEPS = G * B
TOK = B * S
HALF = TOK // 2
SCALE = float(HD) ** -0.5
RMS_EPS = 1e-6
LN_EPS = 1e-5
FF = 1376
QF = FF // 4
KT = [128, 128, QF - 256]
NT = 4 * len(KT)
LORA = 0.5

FIRST_CROSS = {STEPS + 1: -2, STEPS + 2: -1}
FF_EARLY = {STEPS: (0, 1), STEPS + 1: (4, 5)}
FF_LATE = {STEPS: (2, 3)}
FF_XS = {STEPS - 2: (0, 1), STEPS - 1: (2, 3), STEPS: (4, 5), STEPS + 1: (6,), STEPS + 2: (7,)}
FF_TURN = {1: 6, 3: 7}
FF_LORA = 6

B_S, B_T, B_O, B_Y, B_P0, B_P1 = 0, 2, 4, 5, 6, 7


def f32(ap):
    return ap.bitcast(F32)


def need(eng, sem, count):
    if isinstance(count, int) and count <= 0:
        return
    eng.wait_ge(sem, count)


def live(g, b, shift):
    return not isinstance(g, int) or 0 <= B * g + b + shift < STEPS


def build(nc, t):
    with ExitStack() as top:
        def alloc(scope, name, shape, dt=F32):
            return scope.enter_context(nc.sbuf_tensor(name, shape, dt))

        def sem(name):
            return top.enter_context(nc.semaphore(name))

        acc = alloc(top, "acc", [P, B, D])
        ident = alloc(top, "ident", [P, P])
        mhalf = alloc(top, "mhalf", [P, 4])
        eps = alloc(top, "eps", [P, 2])
        lows = alloc(top, "lows", [P, 1])
        bn6 = alloc(top, "bn6", [P, B, 6])
        mv = alloc(top, "mv", [P, B, 2])
        ve = alloc(top, "ve", [P, B])
        rstd = alloc(top, "rstd", [P, B])
        qw = alloc(top, "qw", [P, 1])
        kw = alloc(top, "kw", [P, 1])
        qkw = alloc(top, "qkw", [P, 1])
        ps = top.enter_context(nc.psum_tensor("ps", [P, 8, 512], F32))

        attn = ExitStack()
        xH = alloc(attn, "xH", [P, NC, TOK], F32R)
        xL = alloc(attn, "xL", [P, NC, TOK], F32R)
        cH = alloc(attn, "cH", [P, NC, TOK], F32R)
        cL = alloc(attn, "cL", [P, NC, TOK], F32R)
        QH = alloc(attn, "QH", [P, 2, HPG, HALF], F32R)
        QL = alloc(attn, "QL", [P, 2, HPG, HALF], F32R)
        wqH = alloc(attn, "wqH", [P, HPG, NC, HD], F32R)
        wqL = alloc(attn, "wqL", [P, HPG, NC, HD], F32R)
        wkH = alloc(attn, "wkH", [P, NC, 2 * HD], F32R)
        wkL = alloc(attn, "wkL", [P, NC, 2 * HD], F32R)
        woH = alloc(attn, "woH", [P, HPG, D], F32R)
        woL = alloc(attn, "woL", [P, HPG, D], F32R)
        KHL = alloc(attn, "KHL", [P, 2, 2, 2 * S], F32R)
        VH = alloc(attn, "VH", [P, 4, 2, HD], F32R)
        VL = alloc(attn, "VL", [P, 4, 2, HD], F32R)
        rawq = alloc(attn, "rawq", [P, HPG, NC, HD])
        rawko = alloc(attn, "rawko", [P, HPG * D])
        pr = alloc(attn, "pr", [P, HPG, 2 * S])
        PH = [alloc(attn, "PH0", [P, HPG * S], F32R)]
        PL = [alloc(attn, "PL0", [P, HPG * S], F32R)]
        OH = alloc(attn, "OH", [P, 2, HPG * S], F32R)
        OL = alloc(attn, "OL", [P, 2, HPG * S], F32R)
        kraw = alloc(attn, "kraw", [P, 2, 2, HD])
        nmax = alloc(attn, "nmax", [P, HPG])
        nbias = alloc(attn, "nbias", [P, HPG])
        sums = alloc(attn, "sums", [P, HPG])
        rsum = alloc(attn, "rsum", [P, HPG])
        xraw = acc.rearrange("p b d -> p (b d)").rearrange("p (c n) -> p c n", c=NC)
        only1 = ExitStack()
        sc_b = alloc(only1, "sc_b", [P, HPG * S])
        bias = alloc(only1, "bias", [P, HPG * S])
        rawc = alloc(only1, "rawc", [P, 2, HALF])
        only1.close()
        only2 = ExitStack()
        PH.append(alloc(only2, "PH1", [P, HPG * S], F32R))
        PL.append(alloc(only2, "PL1", [P, HPG * S], F32R))
        kn = alloc(only2, "kn", [P, 2, HD])
        qraw = alloc(only2, "qraw", [P, HPG * HD])
        qss = alloc(only2, "qss", [P, HPG])
        junk = alloc(only2, "junk", [P, 2, HD])
        kss = alloc(only2, "kss", [P, 2, 2])
        kms = alloc(only2, "kms", [P, 2])
        krs = alloc(only2, "krs", [P, 2])
        qms = alloc(only2, "qms", [P, HPG])
        qsc = alloc(only2, "qsc", [P, 2, HPG])
        only2.close()
        attn.close()

        wraw = alloc(top, "wraw", [P, 2, NT * P])
        wgH = alloc(top, "wgH", [P, 2, NT * P], F32R)
        wgL = alloc(top, "wgL", [P, 2, NT * P], F32R)
        w2raw = alloc(top, "w2raw", [P, 3, D])
        w2H = alloc(top, "w2H", [P, 3, D], F32R)
        w2L = alloc(top, "w2L", [P, 3, D], F32R)
        apad = alloc(top, "apad", [P, NC, P])
        xs = alloc(top, "xs", [P, B, P])
        tt = alloc(top, "tt", [P, TOK], F32R)
        x2T = alloc(top, "x2T", [P, NC, TOK])
        xsH = alloc(top, "xsH", [P, TOK], F32R)
        xsL = alloc(top, "xsL", [P, TOK], F32R)
        tt2 = alloc(top, "tt2", [P, TOK], F32R)
        b2raw = alloc(top, "b2raw", [P, D])
        bb2 = alloc(top, "bb2", [P, D], F32R)
        braw = alloc(top, "braw", [P, 2, NT * P])
        bb = alloc(top, "bb", [P, 2, NT * P], F32R)
        a2raw = alloc(top, "a2raw", [P, NT, P])
        a2A = alloc(top, "a2A", [P, NT, P], F32R)
        a2B = alloc(top, "a2B", [P, NT, P], F32R)
        gate = alloc(top, "gate", [P, 2, HALF])
        mid = alloc(top, "mid", [P, 3, HALF])
        midH = alloc(top, "midH", [P, 2, HALF], F32R)
        midL = alloc(top, "midL", [P, 2, HALF], F32R)
        hs = alloc(top, "hs", [P, 3, HALF])
        hsH = alloc(top, "hsH", [P, 3, TOK], F32R)
        hsL = alloc(top, "hsL", [P, 3, TOK], F32R)

        def pair(name):
            return [sem(f"{name}{a}") for a in range(2)]
        q_done, kv_done, kt_done, sc_done = pair("q_done"), pair("kv_done"), pair("kt_done"), pair("sc_done")
        pt_done, pv_done, o_done = pair("pt_done"), pair("pv_done"), pair("o_done")
        act_qraw, qt_done, act_qt = sem("act_qraw"), sem("qt_done"), sem("act_qt")
        act_kv, act_k, act_p, act_exp, act_q, act_o = (pair(n) for n in (
            "act_kv", "act_k", "act_p", "act_exp", "act_q", "act_o"))
        dve_v, dve_k, dve_max, dve_p, dve_rs, dve_q, dve_o, dve_y = (pair(n) for n in (
            "dve_v", "dve_k", "dve_max", "dve_p", "dve_rs", "dve_q", "dve_o", "dve_y"))
        dve_bias, dve_add, dve_nm, dve_qms = sem("dve_bias"), sem("dve_add"), sem("dve_nm"), sem("dve_qms")
        pool_p = pair("pool_p")
        pool_kms, pool_krs, pool_k, pool_q = sem("pool_kms"), sem("pool_krs"), sem("pool_k"), sem("pool_q")
        in_q = [sem(f"in_q{i}") for i in range(HPG)]
        in_kv, in_o, in_bias = sem("in_kv"), sem("in_o"), sem("in_bias")
        in_x = [sem(f"in_x{i}") for i in range(2 * NC)]
        in_acc, in_w = sem("in_acc"), sem("in_w")
        in_c = [sem(f"in_c{i}") for i in range(2)]
        act_wq, act_wkv, act_wo = sem("act_wq"), sem("act_wkv"), sem("act_wo")
        pool_wq, pool_wo, dve_wkv, dve_wo = sem("pool_wq"), sem("pool_wo"), sem("dve_wkv"), sem("dve_wo")
        dve_wq = sem("dve_wq")
        act_x, dve_x, act_c, pool_c = sem("act_x"), sem("dve_x"), sem("act_c"), sem("pool_c")
        lows_ok = sem("lows_ok")
        z_id, id_ok, half_ok, qkw_ok = sem("z_id"), sem("id_ok"), sem("half_ok"), sem("qkw_ok")
        ln_bn, ln_mv, ln_ve, ln_rs, ln_ok = pair("ln_bn"), pair("ln_mv"), pair("ln_ve"), pair("ln_rs"), pair("ln_ok")
        lnt_done, act_lnt, dve_lnt = sem("lnt_done"), sem("act_lnt"), sem("dve_lnt")

        in_ff = [sem(f"in_ff{i}") for i in range(7)]
        ff_xs, ff_t_done, ff_x2T, ff_xsH, ff_xsL = sem("ff_xs"), sem("ff_t_done"), sem("ff_x2T"), sem("ff_xsH"), sem("ff_xsL")
        ff_wH, ff_wL, ff_w2H, ff_w2L = sem("ff_wH"), sem("ff_wL"), sem("ff_w2H"), sem("ff_w2L")
        zero_a2, ff_a2H, ff_a2L, ff_midH, ff_midL = (sem(n) for n in ("zero_a2", "ff_a2H", "ff_a2L", "ff_midH", "ff_midL"))
        ff_bH, ff_bL, ff_b2H, ff_b2L = sem("ff_bH"), sem("ff_bL"), sem("ff_b2H"), sem("ff_b2L")
        lora_done, ff_ttH, ff_ttL = sem("lora_done"), sem("ff_ttH"), sem("ff_ttL")
        up_done, ff_gate, ff_mid, ff_hs = sem("up_done"), sem("ff_gate"), sem("ff_mid"), sem("ff_hs")
        lora2_done, ff_tt2H, ff_tt2L = sem("lora2_done"), sem("ff_tt2H"), sem("ff_tt2L")
        ff_hsH, ff_hsL, down_done, ff_y = sem("ff_hsH"), sem("ff_hsL"), sem("down_done"), sem("ff_y")
        l3_bn, l3_mv, l3_ve, l3_rs, l3_ok, out_ok = (sem(n) for n in ("l3_bn", "l3_mv", "l3_ve", "l3_rs", "l3_ok", "out_ok"))

        def steps(eng, step, last):
            for s in range(-4, B):
                step(0, s // B, s % B)
            with eng.Fori(1, G - 1) as g:
                for b in range(B):
                    step(0, g, b)
            for s in range(STEPS - B, STEPS + 4):
                step(0, s // B, s % B)
                if s in FIRST_CROSS:
                    step(1, -1, B + FIRST_CROSS[s])
            for s in range(0, B):
                step(1, 0, s)
            with eng.Fori(1, G - 1) as g:
                for b in range(B):
                    step(1, g, b)
            for s in range(STEPS - B, last):
                step(1, s // B, s % B)

        def q_bank(g, b):
            return (B_P0, B_Y, B_O, B_S)[b - 4] if isinstance(g, int) and g < 0 else B_P0

        def turn_banks(b):
            return (B_P0, B_P1) if b % 2 == 0 or b == 7 else (B_S, B_S + 1)

        def q_live(a, g, b):
            return live(g, b, 4 if a == 0 else 2)

        def q_block(g, b):
            return g + (b + 4) // B, (b + 4) // 4 % 2, b % 4

        block = top.enter_context(nc.Block())

        @block.sync
        def _(sp):
            def load_q(w, m, first=False):
                if not first:
                    sp.wait_ge(dve_wq if m < 2 else pool_wq, 2 * (w - 1) + m % 2 + 1)
                sp.dma_start(rawq[:, m], t["wq"][w, m]).then_inc(in_q[m], 16)

            def load_kv(w):
                need(sp, dve_wo, 2 * w)
                need(sp, pool_wo, 2 * w)
                sp.dma_start(rawko[:, 0:NC * 2 * HD], t["wkv"][w]).then_inc(in_kv, 16)

            def load_o(w):
                sp.wait_ge(dve_wkv, w + 1)
                sp.dma_start(rawko[:, :], t["wo"][w]).then_inc(in_o, 16)

            def load_bias(g):
                need(sp, dve_add, B * g)
                sp.dma_start(bias[:, :], t["bias"][g]).then_inc(in_bias, 16)

            load_q(0, 0, True)
            for i in range(2 * NC):
                n, c = i // NC, i % NC
                cols = slice(n * HALF, (n + 1) * HALF)
                sp.dma_start(xraw[:, c, cols], t["xT"][c][:, cols]).then_inc(in_x[i], 16)
                if i == NC - 1:
                    load_q(0, 1, True)
                    load_kv(0)
            load_q(0, 2, True)
            load_q(0, 3, True)
            load_bias(0)
            sp.wait_ge(dve_x, 2 * NC)
            sp.dma_start(acc[:, :, :], t["x"]).then_inc(in_acc, 16)
            sp.dma_start(qw[:, :], t["qw"]).then_inc(in_w, 16)
            sp.dma_start(kw[:, :], t["kw"]).then_inc(in_w, 16)

            def group(a, w, g, more):
                load_o(w)
                if more:
                    load_q(w + 1, 0)
                    load_q(w + 1, 1)
                    load_q(w + 1, 2)
                    load_q(w + 1, 3)
                    load_kv(w + 1)

            group(0, 0, 0, True)
            load_bias(1)
            with sp.Fori(1, G - 1) as g:
                group(0, g, g, True)
                load_bias(g + 1)
            def load_context(j):
                need(sp, pool_c, j - 1)
                sp.dma_start(rawc[:, j % 2], t["cT"][j // 2][:, (j % 2) * HALF:(j % 2 + 1) * HALF]).then_inc(in_c[j % 2], 16)
            load_context(0)
            load_context(1)
            group(0, G - 1, G - 1, True)
            for j in range(2, 2 * NC):
                load_context(j)
            with sp.Fori(G, 2 * G - 1) as w:
                group(1, w, w, True)
            group(1, 2 * G - 1, G - 1, False)

            sp.wait_ge(kv_done[1], STEPS)
            for i in range(2):
                sp.dma_start(wraw[:, i], t["w13"][i]).then_inc(in_ff[i], 16)
            for i in range(2):
                sp.dma_start(braw[:, i], t["b13"][i]).then_inc(in_ff[3], 16)
            sp.dma_start(apad[:, :, :], t["apad"]).then_inc(in_ff[2], 16)
            for k in range(3):
                sp.dma_start(w2raw[0:KT[k], k, :], t["w2T"][128 * k:128 * k + KT[k], :]).then_inc(in_ff[6], 16)
            sp.wait_ge(sc_done[1], STEPS)
            sp.dma_start(b2raw[:, :], t["b2T"]).then_inc(in_ff[4], 16)
            sp.wait_ge(o_done[1], STEPS)
            sp.dma_start(a2raw[:, :, :], t["a2pad"]).then_inc(in_ff[5], 16)
            for b in range(B):
                sp.wait_ge(l3_ok, b + 1)
                sp.dma_start(t["out"][b], acc[:, b, :]).then_inc(out_ok, 16)
            sp.wait_ge(out_ok, 16 * B)

        @block.tensor
        def _(pe):
            def parts(lH, lL, rH, rL):
                return ((lH, rH), (lH, rL), (lL, rH))

            def project_q_heads(g, b):
                s2 = B * g + b + 2
                bb_ = (b + 2) % B
                if bb_ == 0:
                    pe.wait_ge(dve_wq, 2 * (g + (b + 2) // B + G + 1))
                    pe.wait_ge(pool_wq, 2 * (g + (b + 2) // B + G + 1))
                if isinstance(g, int) and g < 0:
                    pe.wait_ge(dve_k[0], STEPS)
                    need(pe, act_q[1], s2)
                if isinstance(g, int) and s2 < B:
                    pe.wait_ge(dve_lnt, s2 + 1)
                need(pe, dve_k[1], s2 - 1)
                tok = slice(bb_ * S, (bb_ + 1) * S)
                for c in range(NC):
                    for i, (l, r) in enumerate(parts(xH[:, c, tok], xL[:, c, tok], wqH[:, :, c, :], wqL[:, :, c, :])):
                        mm = pe.matmul(ps[:, B_P0, :], l, r, start=c == 0 and i == 0, stop=c == NC - 1 and i == 2)
                mm.then_inc(q_done[1], 1)

            def turn_q(g, b):
                s = B * g + b
                pe.wait_ge(act_qraw, s + 3)
                if isinstance(g, int) and s == -2:
                    pe.wait_ge(dve_p[0], STEPS)
                if isinstance(g, int) and s <= 0:
                    need(pe, dve_q[1], s + 2)
                for h in range(HPG):
                    mm = pe.transpose(ps[:, B_T, h * S:(h + 1) * S], qraw[:, h * HD:(h + 1) * HD], ident[:, :])
                mm.then_inc(qt_done, 1)

            def project_q(a, g, b):
                gq, half, m = q_block(g, b)
                n = B * g + b + 4
                s = B * g + b
                if half == 0:
                    pe.wait_ge(dve_wq if m < 2 else pool_wq, 2 * gq + m % 2 + 1)
                need(pe, dve_k[a], s + 1)
                if isinstance(g, int) and n == 4:
                    pe.wait_ge(dve_q[a], 4)
                if a == 0 and isinstance(g, int) and n in (0, 4):
                    pe.wait_ge(dve_x, NC * (1 + half))
                for c in range(NC):
                    for i, (l, r) in enumerate(parts(wqH[:, m, c], wqL[:, m, c], xH[:, c, half * HALF:(half + 1) * HALF],
                                                     xL[:, c, half * HALF:(half + 1) * HALF])):
                        mm = pe.matmul(ps[:, q_bank(g, b), :], l, r, start=c == 0 and i == 0, stop=c == NC - 1 and i == 2)
                mm.then_inc(q_done[a], 1)

            def project_kv(a, g, b):
                s2 = B * g + b + 2
                bb_ = (b + 2) % B
                if bb_ == 0:
                    pe.wait_ge(dve_wkv, g + (b + 2) // B + G * a + 1)
                need(pe, dve_v[a], s2)
                if a == 0 and isinstance(g, int) and s2 == 0:
                    pe.wait_ge(dve_x, NC)
                if a == 1 and isinstance(g, int) and s2 == 0:
                    pe.wait_ge(pool_c, 2 * NC)
                    pe.wait_ge(dve_v[0], STEPS)
                if a == 1 and isinstance(g, int) and s2 < B:
                    pe.wait_ge(dve_lnt, s2 + 1)
                tiles = ((xH, xL),) if a == 0 else ((cH, cL), (xH, xL))
                for j, (sH, sL) in enumerate(tiles):
                    for c in range(NC):
                        tok = slice(bb_ * S, (bb_ + 1) * S)
                        for i, (l, r) in enumerate(parts(sH[:, c, tok], sL[:, c, tok], wkH[:, c, :], wkL[:, c, :])):
                            mm = pe.matmul(ps[:, B_P1, j * 2 * HD:(j + 1) * 2 * HD], l, r,
                                           start=c == 0 and i == 0, stop=c == NC - 1 and i == 2)
                mm.then_inc(kv_done[a], 1)

            def turn_keys(a, g, b):
                s1 = B * g + b + 1
                par = (b + 1) % 2
                if a == 0:
                    pe.wait_ge(act_kv[0], s1 + 1)
                else:
                    pe.wait_ge(pool_k, s1 + 1)
                if a == 1:
                    pe.wait_ge(act_q[1], s1 + 2 if live(g, b, 2) else STEPS)
                elif isinstance(g, int) and g < 0:
                    pe.wait_ge(dve_q[0], 1)
                else:
                    pe.wait_ge(dve_q[0], s1 + 4 if live(g, b, 4) else STEPS)
                for j in range(a + 1):
                    src = kraw[:, par, 0] if a == 0 else kn[:, j]
                    mm = pe.transpose(ps[:, B_P0, j * S:(j + 1) * S], src, ident[:, :])
                mm.then_inc(kt_done[a], 1)

            def scores(a, g, b):
                s = B * g + b
                half, tok = b // 4, slice((b % 4) * S, (b % 4 + 1) * S)
                if a == 1:
                    pe.wait_ge(dve_q[1], s + 1)
                    half, tok = b % 2, slice(0, S)
                elif b % 4 == 0:
                    pe.wait_ge(dve_q[0], s + 4)
                pe.wait_ge(dve_k[a], s + 1)
                need(pe, dve_add if a == 0 else act_exp[1], s)
                n = S * (a + 1)
                for h in range(HPG):
                    out = ps[:, B_S + h // 2, h % 2 * 256:h % 2 * 256 + 256]
                    if a == 0:
                        pe.matmul(out, QH[:, half, h, tok], KHL[:, b % 2, :, 0:n], start=True, stop=False,
                                  skip_group_check=True)
                        mm = pe.matmul(out[:, 0:n], QL[:, half, h, tok], KHL[:, b % 2, 0, 0:n], start=False, stop=True,
                                       skip_group_check=True)
                    else:
                        for i, (l, r) in enumerate(parts(QH[:, half, h, tok], QL[:, half, h, tok],
                                                         KHL[:, b % 2, 0], KHL[:, b % 2, 1])):
                            mm = pe.matmul(out, l, r, start=i == 0, stop=i == 2)
                mm.then_inc(sc_done[a], 1)

            def turn_probs(a, g, b):
                s = B * g + b
                pe.wait_ge(pool_p[a], s)
                if a == 1:
                    pe.wait_ge(dve_q[1], s + 2 if live(g, b, 1) else STEPS)
                if a == 1 and isinstance(g, int) and s == 1:
                    pe.wait_ge(dve_lnt, B)
                for j in range(a + 1):
                    for h in range(HPG):
                        mm = pe.transpose(ps[:, B_T + j, h * S:(h + 1) * S], pr[:, h, j * S:(j + 1) * S], ident[:, :])
                mm.then_inc(pt_done[a], 1)

            def weigh_values(a, g, b):
                s = B * g + b
                v = (b - 1) % 4
                pe.wait_ge(dve_p[a], s)
                pe.wait_ge(dve_v[a], s)
                need(pe, dve_o[a], s - 1)
                for j in range(a + 1):
                    for i, (l, r) in enumerate(parts(VH[:, v, j], VL[:, v, j], PH[j][:, :], PL[j][:, :])):
                        mm = pe.matmul(ps[:, B_O, :], l, r, start=j == 0 and i == 0, stop=j == a and i == 2)
                mm.then_inc(pv_done[a], 1)

            def project_out(a, g, b):
                s = B * g + b
                par = b % 2
                pe.wait_ge(dve_o[a], s - 1)
                need(pe, dve_y[a], s - 2)
                for h in range(HPG):
                    if b == 2:
                        pe.wait_ge(dve_wo if h < 2 else pool_wo, 2 * (g + G * a) + h % 2 + 1)
                    tok = slice(h * S, (h + 1) * S)
                    for i, (l, r) in enumerate(parts(OH[:, par, tok], OL[:, par, tok], woH[:, h], woL[:, h])):
                        mm = pe.matmul(ps[:, B_Y, :], l, r, start=h == 0 and i == 0, stop=h == HPG - 1 and i == 2)
                mm.then_inc(o_done[a], 1)

            def turn_norm(b):
                pe.wait_ge(ln_ok[0], b + 1)
                need(pe, dve_lnt, b)
                for c in range(NC):
                    mm = pe.transpose(ps[:, B_T + 1, c * P:(c + 1) * P], acc[:, b, c * P:(c + 1) * P], ident[:, :])
                mm.then_inc(lnt_done, 1)

            def turn_x2(b):
                pe.wait_ge(ff_xs, b + 1)
                if b == 0:
                    pe.wait_ge(dve_k[1], STEPS)
                    pe.wait_ge(dve_v[1], STEPS)
                    pe.wait_ge(act_exp[1], STEPS)
                need(pe, ff_xsL, b - 1 if b < 7 else b)
                one, two = turn_banks(b)
                for c in range(NC):
                    pe.transpose(ps[:, one, c * P:(c + 1) * P], acc[:, b, c * P:(c + 1) * P], ident[:, :])
                pe.transpose(ps[:, two, 0:P], xs[:, b, :], ident[:, :]).then_inc(ff_t_done, 1)

            def lora_in(n):
                pe.wait_ge(in_ff[2], 16)
                pe.wait_ge(ff_x2T, B // 2 * (n + 1))
                pe.wait_ge(dve_o[1] if n == 0 else dve_y[1], STEPS)
                for c in range(NC):
                    mm = pe.matmul(ps[:, B_O + n, :], apad[:, c, :], x2T[:, c, n * HALF:(n + 1) * HALF],
                                   start=c == 0, stop=c == NC - 1)
                mm.then_inc(lora_done, 1)

            def step(a, g, b):
                static = isinstance(g, int)
                s = B * g + b
                tail = a == 0 and static and s >= STEPS - 4
                early_kv = static and (s == -2 and a == 0 or -2 <= s < 2 and a == 1)
                if live(g, b, 0):
                    scores(a, g, b)
                if tail and live(g, b, 1):
                    turn_keys(a, g, b)
                if live(g, b, -1):
                    turn_probs(a, g, b)
                if early_kv and a == 0:
                    project_kv(a, g, b)
                if q_live(a, g, b):
                    if a == 0:
                        project_q(a, g, b)
                    else:
                        project_q_heads(g, b)
                if early_kv and a == 1:
                    project_kv(a, g, b)
                if a == 1 and static:
                    for c in FF_EARLY.get(s, ()):
                        turn_x2(c)
                if a == 0 and isinstance(g, int) and B * g + b >= STEPS - 4:
                    turn_norm(B * g + b - (STEPS - 4))
                last = isinstance(g, int) and B * g + b >= STEPS - 4
                if last and live(g, b, -2):
                    project_out(a, g, b)
                if live(g, b, -1):
                    weigh_values(a, g, b)
                if not last and live(g, b, -2):
                    project_out(a, g, b)
                if a == 1 and static:
                    for c in FF_LATE.get(s, ()):
                        turn_x2(c)
                if a == 1 and live(g, b, 2):
                    turn_q(g, b)
                if static and s == -1 and a == 0:
                    project_kv(a, g, b)
                if not tail and live(g, b, 1):
                    turn_keys(a, g, b)
                if live(g, b, 2) and not early_kv and not (static and s == -1 and a == 0):
                    project_kv(a, g, b)

            pe.wait_ge(id_ok, 1)
            steps(pe, step, STEPS + 2)

            lora_in(0)

            def lora2(u):
                n, k = u // NT, u % NT
                rows = KT[k % 3]
                pe.wait_ge(ff_midL, u + 1)
                if u == 0:
                    pe.wait_ge(ff_a2L, 1)
                for i, (l, r) in enumerate(((a2A, midH), (a2B, midL))):
                    x = pe.matmul(ps[:, B_O + n, :], l[0:rows, k, :], r[0:rows, u % 2, :],
                                  start=k == 0 and i == 0, stop=k == NT - 1 and i == 1, skip_group_check=True)
                x.then_inc(lora2_done, 1)

            for n in range(2):
                pe.wait_ge(ff_xsL, 6 if n == 0 else B)
                for k in range(NT):
                    u = n * NT + k
                    rows = KT[k % 3]
                    cols = slice(k * P, k * P + rows)
                    tok = slice(n * HALF, (n + 1) * HALF)
                    need(pe, ff_mid, u - 1)
                    for i in range(2):
                        if u == 0:
                            pe.wait_ge(ff_wL, i + 1)
                        out = ps[0:rows, 2 * (u % 2) + i, :]
                        for j, (l, r) in enumerate(parts(wgH[:, i, cols], wgL[:, i, cols], xsH[:, tok], xsL[:, tok])):
                            pe.matmul(out, l, r, start=j == 0, stop=False)
                        if k == 0 and i == 0:
                            pe.wait_ge(ff_ttL, n + 1)
                        if u == 0:
                            pe.wait_ge(ff_bL, i + 1)
                        mm = pe.matmul(out, bb[:, i, cols], tt[:, tok], start=False, stop=True)
                    mm.then_inc(up_done, 1)
                    if u >= 2:
                        lora2(u - 2)
                    if u in FF_TURN:
                        turn_x2(FF_TURN[u])
                    if u == FF_LORA:
                        lora_in(1)
            pe.wait_ge(ff_w2L, 3)
            pe.wait_ge(ff_b2L, 1)
            for b in range(B):
                if b == 1:
                    lora2(2 * NT - 2)
                    lora2(2 * NT - 1)
                tok = slice(b * S, (b + 1) * S)
                if b % 4 == 0:
                    pe.wait_ge(ff_hsL, 3 * (b // 4 + 1))
                    pe.wait_ge(ff_tt2L, b // 4 + 1)
                need(pe, ff_y, b - 1)
                for k in range(3):
                    rows = KT[k]
                    for i, (l, r) in enumerate(parts(hsH[0:rows, k, tok], hsL[0:rows, k, tok],
                                                     w2H[0:rows, k], w2L[0:rows, k])):
                        pe.matmul(ps[:, 6 + b % 2, :], l, r, start=k == 0 and i == 0, stop=False)
                pe.matmul(ps[:, 6 + b % 2, :], tt2[:, tok], bb2[:, :], start=False, stop=True).then_inc(down_done, 1)

        @block.scalar
        def _(act):
            def high(out, src, scale=1.0):
                return act.activation(out, src, ACT.Copy, scale=scale)

            def split_wq(w, m):
                act.wait_ge(in_q[m], 16 * (w + 1))
                high(wqH[:, m], rawq[:, m]).then_inc(act_wq, 1)

            def split_wkv(w):
                act.wait_ge(in_kv, 16 * (w + 1))
                high(wkH[:, :, :], rawko[:, 0:NC * 2 * HD].rearrange("p (c n) -> p c n", c=NC)).then_inc(act_wkv, 1)

            def split_wo(w):
                act.wait_ge(in_o, 16 * (w + 1))
                for h in range(HPG):
                    high(woH[:, h], rawko[:, h * D:(h + 1) * D]).then_inc(act_wo, 1)

            def take_x2(b):
                one, two = turn_banks(b)
                act.wait_ge(ff_t_done, b + 1)
                act.activation(x2T[:, :, b * S:(b + 1) * S], ps[:, one, :].rearrange("p (c n) -> p c n", c=NC),
                               ACT.Copy).then_inc(ff_x2T, 1)
                high(xsH[:, b * S:(b + 1) * S], ps[:, two, 0:P]).then_inc(ff_xsH, 1)

            def high_keys(a, g, b):
                act.wait_ge(kt_done[a], B * g + b + 2)
                n, par = S * (a + 1), (b + 1) % 2
                high(KHL[:, par, 0, 0:n], ps[:, B_P0, 0:n], 1.0 if a == 0 else qkw[:, 0:1]).then_inc(act_k[a], 1)

            def step(a, g, b):
                s = B * g + b
                w = g + G * a
                refill = not isinstance(g, int) or (0 <= g < G and w + 1 < 2 * G)
                tail = a == 0 and isinstance(g, int) and s >= STEPS - 4
                if a == 1 and isinstance(g, int) and s == -1:
                    act.wait_ge(qkw_ok, 1)
                if live(g, b, 1):
                    act.wait_ge(kv_done[a], s + 2)
                    kv = ps[:, B_P1, 0:(a + 1) * 2 * HD].rearrange("p (j n) -> p j n", n=2 * HD)
                    v, par = (b + 1) % 4, (b + 1) % 2
                    high(VH[:, v, 0:a + 1], kv[:, :, HD:2 * HD])
                    if a == 0:
                        act.activation(kraw[:, par, 0:1], kv[:, :, 0:HD], ACT.Copy).then_inc(act_kv[0], 1)
                    else:
                        act.activation(kraw[:, par, 0:2], kv[:, :, 0:HD], ACT.Copy)
                        for j in range(2):
                            x = act.activation(junk[:, j], kv[:, j, 0:HD], ACT.Square, scale=SCALE, accum_out=kss[:, par, j:j + 1])
                        x.then_inc(act_kv[1], 1)
                if tail and live(g, b, 1):
                    high_keys(a, g, b)
                if b == 6 and refill and not tail:
                    split_wkv(w + 1)
                if live(g, b, -1):
                    act.wait_ge(pt_done[a], s)
                    for j in range(a + 1):
                        x = high(PH[j][:, :], ps[:, B_T + j, :])
                    x.then_inc(act_p[a], 1)
                if a == 0 and tail and s == STEPS:
                    split_wkv(G)
                if a == 1 and isinstance(g, int):
                    for c in FF_EARLY.get(s, ()):
                        take_x2(c)
                if b == 2 and live(g, b, -2):
                    need(act, o_done[a], s - 2)
                    if a == 1 and isinstance(g, int) and g == 0:
                        act.wait_ge(o_done[0], STEPS)
                    split_wo(w)
                if live(g, b, 0):
                    act.wait_ge(dve_max[a], s + 1)
                    for h in range(HPG):
                        if a == 0:
                            x = act.activation(pr[:, h, 0:S], sc_b[:, h * S:(h + 1) * S], ACT.Exp,
                                               bias=nmax[:, h:h + 1], accum_out=sums[:, h:h + 1])
                        else:
                            x = act.activation(pr[:, h, :], ps[:, B_S + h // 2, (h % 2) * 256:(h % 2 + 1) * 256], ACT.Exp,
                                               bias=nbias[:, h:h + 1], scale=qsc[:, b % 2, h:h + 1],
                                               accum_out=sums[:, h:h + 1])
                    x.then_inc(act_exp[a], 1)
                if a == 0 and q_live(a, g, b):
                    _, half, m = q_block(g, b)
                    act.wait_ge(q_done[0], s + 5)
                    high(QH[:, half, m], ps[:, q_bank(g, b), :], SCALE).then_inc(act_q[0], 1)
                if a == 1 and q_live(a, g, b):
                    act.wait_ge(q_done[1], s + 3)
                    need(act, qt_done, s + 2)
                    act.activation(qraw[:, :], ps[:, B_P0, :], ACT.Copy).then_inc(act_qraw, 1)
                    need(act, dve_qms, s + 2)
                    act.wait_ge(act_qraw, s + 3)
                    for h in range(HPG):
                        head = ps[:, B_P0, h * HD:(h + 1) * HD]
                        x = act.activation(head, head, ACT.Square, accum_out=qss[:, h:h + 1])
                    x.then_inc(act_q[1], 1)
                if a == 0 and isinstance(g, int) and s >= STEPS - 4:
                    c = s - (STEPS - 4)
                    act.wait_ge(lnt_done, c + 1)
                    high(xH[:, :, c * S:(c + 1) * S], ps[:, B_T + 1, :].rearrange("p (c n) -> p c n", c=NC)).then_inc(act_lnt, 1)
                if live(g, b, -1):
                    act.wait_ge(pv_done[a], s)
                    need(act, o_done[a], s - 2)
                    high(OH[:, (b - 1) % 2], ps[:, B_O, :]).then_inc(act_o[a], 1)
                if a == 1 and q_live(a, g, b):
                    act.wait_ge(qt_done, s + 3)
                    high(QH[:, b % 2, :, 0:S], ps[:, B_T, :].rearrange("p (h n) -> p h n", h=HPG)).then_inc(act_qt, 1)
                if a == 1 and isinstance(g, int):
                    for c in FF_LATE.get(s, ()):
                        take_x2(c)
                    if s in (STEPS - 1, STEPS):
                        i = s - (STEPS - 1)
                        act.wait_ge(in_ff[i], 16)
                        high(wgH[:, i], wraw[:, i]).then_inc(ff_wH, 1)
                        act.wait_ge(in_ff[3], 16 * 2)
                        high(bb[:, i], braw[:, i]).then_inc(ff_bH, 1)
                if a == 0 and b < 4 and refill:
                    split_wq(w + 1, b)
                if not tail and live(g, b, 1):
                    high_keys(a, g, b)
                if a == 1 and b == 5 and refill:
                    for m in range(HPG):
                        split_wq(w + 1, m)
                if a == 0 and isinstance(g, int) and g == G - 1:
                    act.wait_ge(in_c[b % 2], 16 * (b // 2 + 1))
                    high(cH[:, b // 2, (b % 2) * HALF:(b % 2 + 1) * HALF], rawc[:, b % 2]).then_inc(act_c, 1)

            split_wq(0, 0)
            def split_x(n):
                for c in range(NC):
                    cols = slice(n * HALF, (n + 1) * HALF)
                    act.wait_ge(in_x[n * NC + c], 16)
                    high(xH[:, c, cols], xraw[:, c, cols]).then_inc(act_x, 1)

            split_x(0)
            split_wq(0, 1)
            split_wkv(0)
            split_x(1)
            split_wq(0, 2)
            split_wq(0, 3)
            steps(act, step, STEPS + 2)

            def lora_high(n):
                act.wait_ge(lora_done, n + 1)
                high(tt[:, n * HALF:(n + 1) * HALF], ps[:, B_O + n, :], LORA).then_inc(ff_ttH, 1)

            def split_mid(u):
                rows = KT[u % NT % 3]
                act.wait_ge(ff_mid, u + 1)
                need(act, lora2_done, u - 1)
                high(midH[0:rows, u % 2], mid[0:rows, u % 3]).then_inc(ff_midH, 1)

            def finish_sum(n, k):
                act.wait_ge(ff_hs, n * NT + 9 + k + 1)
                high(hsH[0:KT[k], k, n * HALF:(n + 1) * HALF], hs[0:KT[k], k, :]).then_inc(ff_hsH, 1)

            def finish_t2(n):
                cols = slice(n * HALF, (n + 1) * HALF)
                act.wait_ge(lora2_done, NT * (n + 1))
                high(tt2[:, cols], ps[:, B_O + n, :], LORA).then_inc(ff_tt2H, 1)

            lora_high(0)
            for n in range(2):
                for k in range(NT):
                    u = n * NT + k
                    rows = KT[k % 3]
                    act.wait_ge(up_done, u + 1)
                    need(act, ff_mid, u - 1)
                    act.activation(gate[0:rows, u % 2], ps[0:rows, 2 * (u % 2), :], ACT.Silu).then_inc(ff_gate, 1)
                    if u == 0:
                        act.wait_ge(in_ff[5], 16)
                        act.wait_ge(zero_a2, 1)
                        high(a2A[:, :, :], a2raw[:, :, :])
                        wide = [v[:, :, :].rearrange("p k (q c) -> p k q c", q=4) for v in (a2B, a2raw)]
                        for q in range(4):
                            x = high(wide[0][:, :, q, 0:2], wide[1][:, :, q, 0:2])
                        x.then_inc(ff_a2H, 1)
                    if u >= 1:
                        split_mid(u - 1)
                    if u in FF_TURN:
                        take_x2(FF_TURN[u])
                    if u == FF_LORA:
                        lora_high(1)
                    if 7 <= u < 10:
                        j = u - 7
                        act.wait_ge(in_ff[6], 16 * 3)
                        high(w2H[0:KT[j], j], w2raw[0:KT[j], j]).then_inc(ff_w2H, 1)
                    if u == 10:
                        act.wait_ge(in_ff[4], 16)
                        high(bb2[:, :], b2raw[:, :]).then_inc(ff_b2H, 1)
                    if NT <= u < NT + 3:
                        finish_sum(0, u - NT)
                    if u == NT + 3:
                        finish_t2(0)
            split_mid(2 * NT - 1)
            for k in range(3):
                finish_sum(1, k)
            finish_t2(1)

        @block.vector
        def _(dve):
            def low(out, src, hi):
                return dve.tensor_tensor(out, src, f32(hi), ALU.subtract)

            def split_wkv(w):
                dve.wait_ge(act_wkv, w + 1)
                low(wkL[:, :, :], rawko[:, 0:NC * 2 * HD].rearrange("p (c n) -> p c n", c=NC), wkH[:, :, :]).then_inc(dve_wkv, 1)

            def norm_stats(a, b):
                dve.bn_stats(bn6[:, b, :], acc[:, b, :]).then_inc(ln_bn[a], 1)
                dve.wait_ge(ln_bn[a], b + 1)
                dve.bn_aggr(mv[:, b, :], bn6[:, b, :]).then_inc(ln_mv[a], 1)
                dve.wait_ge(ln_mv[a], b + 1)
                dve.tensor_scalar(ve[:, b:b + 1], mv[:, b, 1:2], LN_EPS, None, ALU.add).then_inc(ln_ve[a], 1)

            def norm_apply(a, b):
                dve.wait_ge(ln_rs[a], b + 1)
                dve.tensor_scalar(acc[:, b, :], acc[:, b, :], mv[:, b, 0:1], rstd[:, b:b + 1],
                                  ALU.subtract, ALU.mult).then_inc(ln_ok[a], 1)

            def take_xs(b):
                dve.wait_ge(ff_xsH, b + 1)
                low(xsL[:, b * S:(b + 1) * S], ps[:, turn_banks(b)[1], 0:P], xsH[:, b * S:(b + 1) * S]).then_inc(ff_xsL, 1)

            def split_wq(w, m):
                dve.wait_ge(act_wq, HPG * w + m + 1)
                low(wqL[:, m], rawq[:, m], wqH[:, m]).then_inc(dve_wq, 1)

            def lora_low(n, out, hi_done, lo_done):
                dve.wait_ge(hi_done, n + 1)
                cols = slice(n * HALF, (n + 1) * HALF)
                dve.scalar_tensor_tensor(out=out[64:128, cols], in0=ps[64:128, B_O + n, :], scalar=LORA,
                                         in1=f32(out[64:128, cols]), op0=ALU.mult, op1=ALU.subtract).then_inc(lo_done, 1)

            def low_up(i):
                dve.wait_ge(ff_wH, i + 1)
                low(wgL[:, i], wraw[:, i], wgH[:, i]).then_inc(ff_wL, 1)

            def by_rows(out, src):
                return dve.scalar_tensor_tensor(out=out, in0=f32(out), scalar=lows[:, 0:1], in1=src, op0=ALU.mult, op1=ALU.add)

            def low_up_b(i):
                dve.wait_ge(ff_bH, i + 1)
                by_rows(bb[:, i], braw[:, i]).then_inc(ff_bL, 1)

            def low_keys(a, g, b):
                dve.wait_ge(act_k[a], B * g + b + 2)
                n, par = S * (a + 1), (b + 1) % 2
                if a == 0:
                    low(KHL[:, par, 1, 0:n], ps[:, B_P0, 0:n], KHL[:, par, 0, 0:n]).then_inc(dve_k[0], 1)
                else:
                    dve.scalar_tensor_tensor(out=KHL[:, par, 1, 0:n], in0=ps[:, B_P0, 0:n], scalar=qkw[:, 0:1],
                                             in1=f32(KHL[:, par, 0, 0:n]), op0=ALU.mult, op1=ALU.subtract).then_inc(dve_k[1], 1)

            def step(a, g, b):
                s = B * g + b
                w = g + G * a
                if a == 1 and isinstance(g, int) and s == STEPS + 2:
                    lora_low(0, tt, ff_ttH, ff_ttL)
                if a == 1 and isinstance(g, int) and s == -2:
                    dve.wait_ge(in_w, 32)
                    dve.tensor_tensor(qkw[:, :], qw[:, :], kw[:, :], ALU.mult).then_inc(qkw_ok, 1)
                if a == 1 and isinstance(g, int) and s == -1:
                    dve.wait_ge(qkw_ok, 1)
                if live(g, b, 1):
                    dve.wait_ge(act_kv[a], s + 2)
                    kv = ps[:, B_P1, 0:(a + 1) * 2 * HD].rearrange("p (j n) -> p j n", n=2 * HD)
                    v = (b + 1) % 4
                    low(VL[:, v, 0:a + 1], kv[:, :, HD:2 * HD], VH[:, v, 0:a + 1]).then_inc(dve_v[a], 1)
                if live(g, b, 0):
                    dve.wait_ge(sc_done[a], s + 1)
                    if a == 0:
                        if b == 0:
                            dve.wait_ge(in_bias, 16 * (g + 1))
                        need(dve, act_exp[0], s)
                        both = ps[:, B_S:B_S + 2, :].rearrange("p j (h i k) -> p (j h) i k", h=2, i=2)
                        shaped = [v[:, :].rearrange("p (h k) -> p h k", h=HPG) for v in (sc_b, bias)]
                        dve.tensor_tensor(shaped[0], both[:, :, 1], shaped[1], ALU.add).then_inc(dve_bias, 1)
                        dve.wait_ge(dve_bias, s + 1)
                        dve.tensor_tensor(shaped[0], both[:, :, 0], shaped[0], ALU.add).then_inc(dve_add, 1)
                        dve.wait_ge(dve_add, s + 1)
                        dve.tensor_reduce(nmax[:, :], sc_b[:, :].rearrange("p (h k) -> p h k", h=HPG), AX.X, ALU.max,
                                          negate=True).then_inc(dve_max[0], 1)
                    else:
                        dve.tensor_reduce(nmax[:, :], ps[:, B_S:B_S + 2, :].rearrange("p j (h k) -> p (j h) k", h=2),
                                          AX.X, ALU.max, negate=True).then_inc(dve_nm, 1)
                        dve.wait_ge(dve_nm, s + 1)
                        dve.wait_ge(pool_q, s + 1)
                        need(dve, act_exp[1], s)
                        dve.tensor_tensor(nbias[:, :], nmax[:, :], qsc[:, b % 2, :], ALU.mult).then_inc(dve_max[1], 1)
                tail = isinstance(g, int) and s >= STEPS - 6
                early_keys = a == 0 and isinstance(g, int) and s >= STEPS - 4
                if early_keys and live(g, b, 1):
                    low_keys(a, g, b)
                if live(g, b, -1):
                    dve.wait_ge(act_p[a], s)
                    for j in range(a + 1):
                        x = low(PL[j][:, :], ps[:, B_T + j, :], PH[j][:, :])
                    x.then_inc(dve_p[a], 1)
                if a == 1 and isinstance(g, int):
                    for c in FF_EARLY.get(s, ()):
                        take_xs(c)
                refill = not isinstance(g, int) or (0 <= g < G and w + 1 < 2 * G)
                if b == 6 and refill and not early_keys:
                    split_wkv(w + 1)
                if a == 0 and early_keys and s == STEPS:
                    split_wkv(G)
                if isinstance(g, int) and s - 3 >= STEPS - B and live(g, b, -3):
                    norm_apply(a, s - 3 - (STEPS - B))
                if a == 1 and isinstance(g, int):
                    for c in FF_XS.get(s, ()):
                        dve.wait_ge(ln_ok[1], c + 1)
                        dve.tensor_reduce(xs[:, c, :], acc[:, c, :].rearrange("p (c f) -> p f c", c=NC), AX.X,
                                          ALU.add).then_inc(ff_xs, 1)
                if b == 2 and live(g, b, -2):
                    for h in range(2):
                        dve.wait_ge(act_wo, HPG * w + h + 1)
                        low(woL[:, h], rawko[:, h * D:(h + 1) * D], woH[:, h]).then_inc(dve_wo, 1)
                if live(g, b, 0):
                    dve.wait_ge(act_exp[a], s + 1)
                    need(dve, pool_p[a], s)
                    dve.reciprocal(rsum[:, :], sums[:, :]).then_inc(dve_rs[a], 1)
                if a == 0 and q_live(a, g, b):
                    _, half, m = q_block(g, b)
                    dve.wait_ge(act_q[0], s + 5)
                    dve.scalar_tensor_tensor(out=QL[:, half, m], in0=ps[:, q_bank(g, b), :], scalar=SCALE, in1=f32(QH[:, half, m]),
                                             op0=ALU.mult, op1=ALU.subtract).then_inc(dve_q[0], 1)
                if a == 0 and isinstance(g, int) and s >= STEPS - 4:
                    c = s - (STEPS - 4)
                    dve.wait_ge(act_lnt, c + 1)
                    low(xL[:, :, c * S:(c + 1) * S], ps[:, B_T + 1, :].rearrange("p (c n) -> p c n", c=NC),
                        xH[:, :, c * S:(c + 1) * S]).then_inc(dve_lnt, 1)
                if live(g, b, -1):
                    dve.wait_ge(act_o[a], s)
                    low(OL[:, (b - 1) % 2], ps[:, B_O, :], OH[:, (b - 1) % 2]).then_inc(dve_o[a], 1)
                if a == 1 and q_live(a, g, b):
                    dve.wait_ge(act_q[1], s + 3)
                    need(dve, pool_q, s + 2)
                    dve.tensor_scalar(qms[:, :], qss[:, :], HD * RMS_EPS, None, ALU.add).then_inc(dve_qms, 1)
                    dve.wait_ge(act_qt, s + 3)
                    low(QL[:, b % 2, :, 0:S], ps[:, B_T, :].rearrange("p (h n) -> p h n", h=HPG),
                        QH[:, b % 2, :, 0:S]).then_inc(dve_q[1], 1)
                if a == 1 and isinstance(g, int):
                    for c in FF_LATE.get(s, ()):
                        take_xs(c)
                    if s == STEPS - 1:
                        low_up(0)
                    if s == STEPS + 1:
                        low_up_b(0)
                if tail and not early_keys and live(g, b, 1):
                    low_keys(a, g, b)
                if live(g, b, -2):
                    bb_ = (b - 2) % B
                    if a == 0 and isinstance(g, int) and s == 2:
                        dve.wait_ge(in_acc, 16)
                    dve.wait_ge(o_done[a], s - 1)
                    need(dve, dve_y[a], s - 2)
                    dve.tensor_tensor(acc[:, bb_, :], ps[:, B_Y, :], acc[:, bb_, :], ALU.add).then_inc(dve_y[a], 1)
                if isinstance(g, int) and s - 2 >= STEPS - B and live(g, b, -2):
                    dve.wait_ge(dve_y[a], s - 1)
                    norm_stats(a, s - 2 - (STEPS - B))
                if a == 1 and isinstance(g, int) and s == STEPS:
                    low_up(1)
                if a == 1 and isinstance(g, int) and s == STEPS + 1:
                    low_up_b(1)
                if not tail and live(g, b, 1):
                    low_keys(a, g, b)
                if a == 0 and b < 2 and refill:
                    split_wq(w + 1, b)
                if a == 1 and b == 5 and refill:
                    split_wq(w + 1, 0)
                    split_wq(w + 1, 1)

            def split_x(n):
                for c in range(NC):
                    cols = slice(n * HALF, (n + 1) * HALF)
                    dve.wait_ge(act_x, n * NC + c + 1)
                    low(xL[:, c, cols], xraw[:, c, cols], xH[:, c, cols]).then_inc(dve_x, 1)

            for q in range(4):
                dve.memset(lows[32 * q:32 * q + 32, :], -float(q % 2)).then_inc(lows_ok, 1)
            split_wq(0, 0)
            split_x(0)
            split_wq(0, 1)
            split_wkv(0)
            split_x(1)
            dve.wait_ge(lows_ok, 4)
            steps(dve, step, STEPS + 3)

            def split_mid(u):
                rows = KT[u % NT % 3]
                dve.wait_ge(ff_midH, u + 1)
                low(midL[0:rows, u % 2], mid[0:rows, u % 3], midH[0:rows, u % 2]).then_inc(ff_midL, 1)

            def finish_sum(n, k):
                cols = slice(n * HALF, (n + 1) * HALF)
                dve.wait_ge(ff_hsH, n * 3 + k + 1)
                low(hsL[0:KT[k], k, cols], hs[0:KT[k], k, :], hsH[0:KT[k], k, cols]).then_inc(ff_hsL, 1)

            for n in range(2):
                for k in range(NT):
                    u = n * NT + k
                    rows = KT[k % 3]
                    dve.wait_ge(ff_gate, u + 1)
                    need(dve, ff_hs, u - 2)
                    need(dve, ff_midL, u - 2)
                    dve.tensor_tensor(mid[0:rows, u % 3], ps[0:rows, 2 * (u % 2) + 1, :], gate[0:rows, u % 2],
                                      ALU.mult).then_inc(ff_mid, 1)
                    if u == 0:
                        dve.wait_ge(ff_a2H, 1)
                        wide = [v[:, :, :].rearrange("p k (q c) -> p k q c", q=4) for v in (a2A, a2raw)]
                        for q in range(4):
                            x = low(wide[0][:, :, q, 2:4], wide[1][:, :, q, 2:4], wide[0][:, :, q, 2:4])
                        x.then_inc(ff_a2L, 1)
                    if u >= 1:
                        split_mid(u - 1)
                    if u in FF_TURN:
                        take_xs(FF_TURN[u])
                    if u == FF_LORA:
                        lora_low(1, tt, ff_ttH, ff_ttL)
                    if 7 <= u < 10:
                        j = u - 7
                        dve.wait_ge(ff_w2H, j + 1)
                        low(w2L[0:KT[j], j], w2raw[0:KT[j], j], w2H[0:KT[j], j]).then_inc(ff_w2L, 1)
                    if u == 10:
                        dve.wait_ge(ff_b2H, 1)
                        by_rows(bb2[:, :], b2raw[:, :]).then_inc(ff_b2L, 1)
                    if NT <= u < NT + 3:
                        finish_sum(0, u - NT)
                    if u == NT + 3:
                        lora_low(0, tt2, ff_tt2H, ff_tt2L)
            split_mid(2 * NT - 1)
            for b in range(B + 1):
                if b == 1:
                    for k in range(3):
                        finish_sum(1, k)
                    lora_low(1, tt2, ff_tt2H, ff_tt2L)
                if b < B:
                    dve.wait_ge(down_done, b + 1)
                    dve.tensor_tensor(acc[:, b, :], ps[:, 6 + b % 2, :], acc[:, b, :], ALU.add).then_inc(ff_y, 1)
                    dve.wait_ge(ff_y, b + 1)
                    dve.bn_stats(bn6[:, b, :], acc[:, b, :]).then_inc(l3_bn, 1)
                    dve.wait_ge(l3_bn, b + 1)
                    dve.bn_aggr(mv[:, b, :], bn6[:, b, :]).then_inc(l3_mv, 1)
                    dve.wait_ge(l3_mv, b + 1)
                    dve.tensor_scalar(ve[:, b:b + 1], mv[:, b, 1:2], LN_EPS, None, ALU.add).then_inc(l3_ve, 1)
                if b >= 1:
                    c = b - 1
                    dve.wait_ge(l3_rs, c + 1)
                    dve.tensor_scalar(acc[:, c, :], acc[:, c, :], mv[:, c, 0:1], rstd[:, c:c + 1],
                                      ALU.subtract, ALU.mult).then_inc(l3_ok, 1)

        @block.gpsimd
        def _(pool):
            def low(out, src, hi):
                return pool.tensor_tensor(out, src, f32(hi), ALU.subtract)

            def split_wq(w, m):
                pool.wait_ge(act_wq, HPG * w + m + 1)
                low(wqL[:, m], rawq[:, m], wqH[:, m]).then_inc(pool_wq, 1)

            def step(a, g, b):
                s = B * g + b
                w = g + G * a
                if b == 2 and live(g, b, -2):
                    for h in range(2, HPG):
                        pool.wait_ge(act_wo, HPG * w + h + 1)
                        low(woL[:, h], rawko[:, h * D:(h + 1) * D], woH[:, h]).then_inc(pool_wo, 1)
                if a == 1 and live(g, b, 1):
                    par = (b + 1) % 2
                    pool.wait_ge(act_kv[1], s + 2)
                    pool.tensor_tensor(kms[:, :], kss[:, par, :], eps[:, :], ALU.add).then_inc(pool_kms, 1)
                    pool.wait_ge(pool_kms, s + 2)
                    pool.tensor_tensor(krs[:, :], kms[:, :], mhalf[:, 0:2], ALU.pow).then_inc(pool_krs, 1)
                    pool.wait_ge(pool_krs, s + 2)
                    need(pool, kt_done[1], s + 1)
                    pool.tensor_tensor(kn[:, :, :], kraw[:, par], krs[:, :].unsqueeze(2).to_broadcast([P, 2, HD]),
                                       ALU.mult).then_inc(pool_k, 1)
                if live(g, b, 0):
                    pool.wait_ge(dve_rs[a], s + 1)
                    n = S * (a + 1)
                    pool.tensor_tensor(pr[:, 0, 0:n], pr[:, 0, 0:n], rsum[:, 0:1].to_broadcast([P, n]), ALU.mult)
                    for h in range(1, HPG):
                        x = pool.tensor_scalar(pr[:, h, 0:n], pr[:, h, 0:n], rsum[:, h:h + 1], 1.0, ALU.mult, ALU.mult)
                    x.then_inc(pool_p[a], 1)
                refill = not isinstance(g, int) or (0 <= g < G and w + 1 < 2 * G)
                if a == 0 and b in (2, 3) and refill:
                    split_wq(w + 1, b)
                if a == 0 and isinstance(g, int) and g == G - 1:
                    pool.wait_ge(act_c, b + 1)
                    cols = slice((b % 2) * HALF, (b % 2 + 1) * HALF)
                    low(cL[:, b // 2, cols], rawc[:, b % 2], cH[:, b // 2, cols]).then_inc(pool_c, 1)
                if a == 1 and q_live(a, g, b):
                    pool.wait_ge(dve_qms, s + 3)
                    pool.tensor_tensor(qsc[:, b % 2, :], qms[:, :], mhalf[:, :], ALU.pow).then_inc(pool_q, 1)
                if a == 1 and b == 5 and refill:
                    for m in range(2, HPG):
                        split_wq(w + 1, m)
                if isinstance(g, int) and s - 2 >= STEPS - B and live(g, b, -2):
                    c = s - 2 - (STEPS - B)
                    pool.wait_ge(ln_ve[a], c + 1)
                    pool.tensor_tensor(rstd[:, c:c + 1], ve[:, c:c + 1], mhalf[:, 0:1], ALU.pow).then_inc(ln_rs[a], 1)

            pool.memset(ident[:, :], 0.0).then_inc(z_id, 1)
            pool.wait_ge(z_id, 1)
            pool.affine_select(out=ident[:, :], in_=ident[:, :], compare_op=ALU.not_equal, fill=1.0, base=0,
                               pattern=[[-1, P]], channel_multiplier=1).then_inc(id_ok, 1)
            pool.memset(eps[:, :], RMS_EPS)
            pool.memset(mhalf[:, :], -0.5).then_inc(half_ok, 1)
            pool.wait_ge(half_ok, 1)
            for m in range(2, HPG):
                split_wq(0, m)
            steps(pool, step, STEPS + 2)

            pool.wait_ge(o_done[1], STEPS)
            pool.memset(f32(a2B[:, :, :]), 0.0).then_inc(zero_a2, 1)
            for n in range(2):
                for k in range(NT):
                    u = n * NT + k
                    rows = KT[k % 3]
                    pool.wait_ge(ff_mid, u + 1)
                    src = mid[0:rows, u % 3]
                    out = hs[0:rows, k % 3]
                    if k < 3:
                        if n == 1:
                            pool.wait_ge(ff_hsL, k + 1)
                        pool.tensor_copy(out, src).then_inc(ff_hs, 1)
                    else:
                        pool.wait_ge(ff_hs, u - 2)
                        pool.tensor_tensor(out, out, src, ALU.add).then_inc(ff_hs, 1)
            for b in range(B):
                pool.wait_ge(l3_ve, b + 1)
                pool.tensor_tensor(rstd[:, b:b + 1], ve[:, b:b + 1], mhalf[:, 0:1], ALU.pow).then_inc(l3_rs, 1)



def kernel(x, ctx_4096, L0_attn_w_qkv, L0_attn_w_o, L0_xattn_Wq, L0_xattn_Wk, L0_xattn_Wv, L0_xattn_Wo,
           L0_xattn_q_norm_w, L0_xattn_k_norm_w, L0_ffn_w1q, L0_ffn_a1, L0_ffn_b1, L0_ffn_w3q, L0_ffn_a3, L0_ffn_b3,
           L0_ffn_w2q, L0_ffn_a2, L0_ffn_b2):
    import concourse.bacc as bacc
    from concourse.bass_utils import run_bass_kernel_spmd

    def arr(v):
        return np.asarray(v)

    def columns(w, n):
        return w.reshape(NC, P, n, HD).transpose(2, 1, 0, 3)

    w_qkv = arr(L0_attn_w_qkv)
    q1, k1, v1 = w_qkv[:, :G * HPG * HD], w_qkv[:, G * HPG * HD:G * (HPG + 1) * HD], w_qkv[:, G * (HPG + 1) * HD:]
    wq = np.stack([columns(q1, G * HPG), columns(arr(L0_xattn_Wq), G * HPG)]).reshape(2 * G, HPG, P, NC, HD)
    wkv = np.stack([np.concatenate([columns(k, G), columns(v, G)], axis=3)
                    for k, v in ((k1, v1), (arr(L0_xattn_Wk), arr(L0_xattn_Wv)))]).reshape(2 * G, P, NC * 2 * HD)
    wo = np.stack([arr(L0_attn_w_o), arr(L0_xattn_Wo)]).reshape(2 * G, HPG, HD, D).transpose(0, 2, 1, 3).reshape(2 * G, P, HPG * D)

    slope = ((2.0 ** (-8.0 / (G * HPG))) ** np.arange(1, G * HPG + 1, dtype=np.float32)).astype(np.float32)
    rel = np.arange(S)[:, None] - np.arange(S)[None, :]
    dist = np.sqrt(np.maximum(rel, 0).astype(np.float32))
    bias = np.where(rel[None] >= 0, -slope[:, None, None] * dist, np.float32(-1e30)).astype(np.float32)
    bias = bias.reshape(G, HPG, S, S).transpose(0, 2, 1, 3).reshape(G, S, HPG * S)

    def hidden_tiles(w):
        out = np.zeros(w.shape[:-1] + (NT, P), w.dtype)
        for k in range(NT):
            at = k // 3 * QF + k % 3 * P
            out[..., k, :KT[k % 3]] = w[..., at:at + KT[k % 3]]
        return out

    def rows(w, *places):
        out = np.zeros((4, 32, w.shape[1]), w.dtype)
        for i in places:
            out[:, 2 * i:2 * i + 2] = w
        return out.reshape(P, -1)

    def copies(*factors):
        out = np.zeros((factors[0].shape[1], 4, 32), factors[0].dtype)
        for i, f in enumerate(factors):
            out[:, :, 2 * i:2 * i + 2] = f.T[:, None, :]
        return out.reshape(-1, P)

    w13 = np.stack([hidden_tiles(arr(w).T).reshape(P, NT * P) for w in (L0_ffn_w1q, L0_ffn_w3q)])
    b13 = np.stack([rows(hidden_tiles(arr(w).T).reshape(2, NT * P), i) for i, w in enumerate((L0_ffn_b1, L0_ffn_b3))])
    b2T = rows(arr(L0_ffn_b2).T, 0, 1)
    apad = copies(arr(L0_ffn_a1), arr(L0_ffn_a3)).reshape(NC, P, P).transpose(1, 0, 2)
    a2pad = hidden_tiles(copies(arr(L0_ffn_a2), arr(L0_ffn_a2)).T).transpose(2, 1, 0)
    data = {
        "xT": arr(x).reshape(TOK, D).T.reshape(NC, P, TOK), "x": arr(x).transpose(1, 0, 2),
        "cT": arr(ctx_4096).reshape(TOK, D).T.reshape(NC, P, TOK),
        "wq": wq, "wkv": wkv, "wo": wo, "bias": bias,
        "qw": arr(L0_xattn_q_norm_w).reshape(P, 1), "kw": arr(L0_xattn_k_norm_w).reshape(P, 1),
        "w13": w13, "b13": b13, "apad": apad, "a2pad": a2pad,
        "w2T": arr(L0_ffn_w2q).T, "b2T": b2T,
    }
    data = {n: np.ascontiguousarray(v) for n, v in data.items()}
    nc = bacc.Bacc("TRN2", target_bir_lowering=False, num_devices=1)
    t = {n: nc.dram_tensor(f"in_{n}", v.shape, F32, kind="ExternalInput").ap() for n, v in data.items()}
    t["out"] = nc.dram_tensor("out", (B, S, D), F32, kind="ExternalOutput").ap()
    build(nc, t)
    r = run_bass_kernel_spmd(nc, [{f"in_{n}": v for n, v in data.items()}], core_ids=[0])
    return r.results[0]["out"]
```

```python
from contextlib import ExitStack

import numpy as np

import concourse.bass as bass
from concourse import mybir

F32 = mybir.dt.float32
F32R = mybir.dt.float32r
ACT = mybir.ActivationFunctionType
ALU = mybir.AluOpType
AX = mybir.AxisListType

P = 128
B = 8
S = 128
D = 512
NC = D // P
HD = 128
G = 8
HPG = 4
STEPS = G * B
TOK = B * S
HALF = TOK // 2
SCALE = float(HD) ** -0.5
RMS_EPS = 1e-6
LN_EPS = 1e-5
FF = 1376
QF = FF // 4
KT = [128, 128, QF - 256]
NT = 4 * len(KT)
LORA = 0.5

FIRST_CROSS = {STEPS + 1: -2, STEPS + 2: -1}
FF_EARLY = {STEPS: (0, 1)}
FF_LATE = {STEPS: (2, 3), STEPS + 1: (4, 5)}
FF_XS = {STEPS - 2: (0, 1), STEPS - 1: (2, 3), STEPS: (4, 5), STEPS + 1: (6,), STEPS + 2: (7,)}
FF_TURN = {1: 6, 3: 7}
FF_LORA = 6

WARM_UP = 18

WQ_ORDER = (2, 3, 0, 1)

B_S, B_T, B_O, B_Y, B_P0, B_P1 = 0, 2, 4, 5, 6, 7


def f32(ap):
    return ap.bitcast(F32)


def need(eng, sem, count):
    if isinstance(count, int) and count <= 0:
        return
    eng.wait_ge(sem, count)


def peeled(g):
    return isinstance(g, int)


def live(g, b, shift):
    return not peeled(g) or 0 <= B * g + b + shift < STEPS


def build(nc, t):
    with ExitStack() as top:
        def alloc(scope, name, shape, dt=F32):
            return scope.enter_context(nc.sbuf_tensor(name, shape, dt))

        def sem(name):
            return top.enter_context(nc.semaphore(name))

        acc = alloc(top, "acc", [P, B, D])
        ident = alloc(top, "ident", [P, P])
        mhalf = alloc(top, "mhalf", [P, 4])
        eps = alloc(top, "eps", [P, 2])
        lows = alloc(top, "lows", [P, 1])
        bn6 = alloc(top, "bn6", [P, B, 6])
        mv = alloc(top, "mv", [P, B, 2])
        ve = alloc(top, "ve", [P, B])
        rstd = alloc(top, "rstd", [P, B])
        qw = alloc(top, "qw", [P, 1])
        kw = alloc(top, "kw", [P, 1])
        qkw = alloc(top, "qkw", [P, 1])
        ps = top.enter_context(nc.psum_tensor("ps", [P, 8, 512], F32))

        attn = ExitStack()
        xH = alloc(attn, "xH", [P, NC, TOK], F32R)
        xL = alloc(attn, "xL", [P, NC, TOK], F32R)
        cH = alloc(attn, "cH", [P, NC, TOK], F32R)
        cL = alloc(attn, "cL", [P, NC, TOK], F32R)
        QH = alloc(attn, "QH", [P, 2, HPG, HALF], F32R)
        QL = alloc(attn, "QL", [P, 2, HPG, HALF], F32R)
        wqH = alloc(attn, "wqH", [P, HPG, NC, HD], F32R)
        wqL = alloc(attn, "wqL", [P, HPG, NC, HD], F32R)
        wkH = alloc(attn, "wkH", [P, NC, 2 * HD], F32R)
        wkL = alloc(attn, "wkL", [P, NC, 2 * HD], F32R)
        woH = alloc(attn, "woH", [P, HPG, D], F32R)
        woL = alloc(attn, "woL", [P, HPG, D], F32R)
        KHL = alloc(attn, "KHL", [P, 2, 2, 2 * S], F32R)
        VH = alloc(attn, "VH", [P, 4, 2, HD], F32R)
        VL = alloc(attn, "VL", [P, 4, 2, HD], F32R)
        rawq = alloc(attn, "rawq", [P, HPG, NC, HD])
        rawko = alloc(attn, "rawko", [P, HPG * D])
        pr = alloc(attn, "pr", [P, HPG, 2 * S])
        PH = [alloc(attn, "PH0", [P, HPG * S], F32R)]
        PL = [alloc(attn, "PL0", [P, HPG * S], F32R)]
        OH = alloc(attn, "OH", [P, 2, HPG * S], F32R)
        OL = alloc(attn, "OL", [P, 2, HPG * S], F32R)
        kraw = alloc(attn, "kraw", [P, 2, 2, HD])
        nmax = alloc(attn, "nmax", [P, HPG])
        nbias = alloc(attn, "nbias", [P, HPG])
        sums = alloc(attn, "sums", [P, HPG])
        rsum = alloc(attn, "rsum", [P, HPG])
        xraw = acc.rearrange("p b d -> p (b d)").rearrange("p (c n) -> p c n", c=NC)
        only1 = ExitStack()
        sc_b = alloc(only1, "sc_b", [P, HPG * S])
        bias = alloc(only1, "bias", [P, HPG * S])
        rawc = alloc(only1, "rawc", [P, 2, HALF])
        only1.close()
        only2 = ExitStack()
        PH.append(alloc(only2, "PH1", [P, HPG * S], F32R))
        PL.append(alloc(only2, "PL1", [P, HPG * S], F32R))
        kn = alloc(only2, "kn", [P, 2, HD])
        qraw = alloc(only2, "qraw", [P, HPG * HD])
        qss = alloc(only2, "qss", [P, HPG])
        junk = alloc(only2, "junk", [P, 2, HD])
        kss = alloc(only2, "kss", [P, 2, 2])
        kms = alloc(only2, "kms", [P, 2])
        krs = alloc(only2, "krs", [P, 2])
        qms = alloc(only2, "qms", [P, HPG])
        qsc = alloc(only2, "qsc", [P, 2, HPG])
        only2.close()
        attn.close()

        wraw = alloc(top, "wraw", [P, 2, NT * P])
        wgH = alloc(top, "wgH", [P, 2, NT * P], F32R)
        wgL = alloc(top, "wgL", [P, 2, NT * P], F32R)
        w2raw = alloc(top, "w2raw", [P, 3, D])
        w2H = alloc(top, "w2H", [P, 3, D], F32R)
        w2L = alloc(top, "w2L", [P, 3, D], F32R)
        apad = alloc(top, "apad", [P, NC, P])
        xs = alloc(top, "xs", [P, B, P])
        tt = alloc(top, "tt", [P, TOK], F32R)
        x2T = alloc(top, "x2T", [P, NC, TOK])
        xsH = alloc(top, "xsH", [P, TOK], F32R)
        xsL = alloc(top, "xsL", [P, TOK], F32R)
        tt2 = alloc(top, "tt2", [P, TOK], F32R)
        b2raw = alloc(top, "b2raw", [P, D])
        bb2 = alloc(top, "bb2", [P, D], F32R)
        braw = alloc(top, "braw", [P, 2, NT * P])
        bb = alloc(top, "bb", [P, 2, NT * P], F32R)
        a2raw = alloc(top, "a2raw", [P, NT, P])
        a2A = alloc(top, "a2A", [P, NT, P], F32R)
        a2B = alloc(top, "a2B", [P, NT, P], F32R)
        gate = alloc(top, "gate", [P, 2, HALF])
        mid = alloc(top, "mid", [P, 3, HALF])
        midH = alloc(top, "midH", [P, 2, HALF], F32R)
        midL = alloc(top, "midL", [P, 2, HALF], F32R)
        hs = alloc(top, "hs", [P, 3, HALF])
        hsH = alloc(top, "hsH", [P, 3, TOK], F32R)
        hsL = alloc(top, "hsL", [P, 3, TOK], F32R)

        def pair(name):
            return [sem(f"{name}{a}") for a in range(2)]
        q_done, kv_done, kt_done, sc_done = pair("q_done"), pair("kv_done"), pair("kt_done"), pair("sc_done")
        pt_done, pv_done, o_done = pair("pt_done"), pair("pv_done"), pair("o_done")
        act_qraw, qt_done, act_qt = sem("act_qraw"), sem("qt_done"), sem("act_qt")
        act_kv, act_k, act_p, act_exp, act_q, act_o = (pair(n) for n in (
            "act_kv", "act_k", "act_p", "act_exp", "act_q", "act_o"))
        dve_v, dve_k, dve_max, dve_p, dve_rs, dve_q, dve_o, dve_y = (pair(n) for n in (
            "dve_v", "dve_k", "dve_max", "dve_p", "dve_rs", "dve_q", "dve_o", "dve_y"))
        dve_bias, dve_add, dve_nm, dve_qms = sem("dve_bias"), sem("dve_add"), sem("dve_nm"), sem("dve_qms")
        pool_p = pair("pool_p")
        pool_kms, pool_krs, pool_k, pool_q = sem("pool_kms"), sem("pool_krs"), sem("pool_k"), sem("pool_q")
        in_q = [sem(f"in_q{i}") for i in range(HPG)]
        in_kv, in_o, in_bias = sem("in_kv"), sem("in_o"), sem("in_bias")
        in_x = [sem(f"in_x{i}") for i in range(2 * NC)]
        in_acc, in_w = sem("in_acc"), sem("in_w")
        in_c = [sem(f"in_c{i}") for i in range(2)]
        act_wq, act_wkv, act_wo = sem("act_wq"), sem("act_wkv"), sem("act_wo")
        pool_wq, pool_wo, dve_wkv, dve_wo = sem("pool_wq"), sem("pool_wo"), sem("dve_wkv"), sem("dve_wo")
        dve_wq = sem("dve_wq")
        act_x, dve_x, act_c, pool_c = sem("act_x"), sem("dve_x"), sem("act_c"), sem("pool_c")
        lows_ok = sem("lows_ok")
        z_id, id_ok, half_ok, qkw_ok = sem("z_id"), sem("id_ok"), sem("half_ok"), sem("qkw_ok")
        ln_bn, ln_mv, ln_ve, ln_rs, ln_ok = pair("ln_bn"), pair("ln_mv"), pair("ln_ve"), pair("ln_rs"), pair("ln_ok")
        lnt_done, act_lnt, dve_lnt = sem("lnt_done"), sem("act_lnt"), sem("dve_lnt")

        in_ff = [sem(f"in_ff{i}") for i in range(7)]
        ff_xs, ff_t_done, ff_x2T, ff_xsH, ff_xsL = sem("ff_xs"), sem("ff_t_done"), sem("ff_x2T"), sem("ff_xsH"), sem("ff_xsL")
        ff_wL = pair("ff_wL")
        ff_wH, ff_w2H, ff_w2L = sem("ff_wH"), sem("ff_w2H"), sem("ff_w2L")
        zero_a2, ff_a2H, ff_a2L, ff_midH, ff_midL = (sem(n) for n in ("zero_a2", "ff_a2H", "ff_a2L", "ff_midH", "ff_midL"))
        ff_bH, ff_bL, ff_b2H, ff_b2L = sem("ff_bH"), sem("ff_bL"), sem("ff_b2H"), sem("ff_b2L")
        lora_done, ff_ttH, ff_ttL = sem("lora_done"), sem("ff_ttH"), sem("ff_ttL")
        up_done, ff_gate, ff_mid, ff_hs = sem("up_done"), sem("ff_gate"), sem("ff_mid"), sem("ff_hs")
        lora2_done, ff_tt2H, ff_tt2L = sem("lora2_done"), sem("ff_tt2H"), sem("ff_tt2L")
        ff_hsH, ff_hsL, down_done, ff_y = sem("ff_hsH"), sem("ff_hsL"), sem("down_done"), sem("ff_y")
        l3_bn, l3_mv, l3_ve, l3_rs, l3_ok, out_ok = (sem(n) for n in ("l3_bn", "l3_mv", "l3_ve", "l3_rs", "l3_ok", "out_ok"))

        def steps(eng, step, last):
            for s in range(-4, B):
                step(0, s // B, s % B)
            with eng.Fori(1, G - 1) as g:
                for b in range(B):
                    step(0, g, b)
            for s in range(STEPS - B, STEPS + 4):
                step(0, s // B, s % B)
                if s in FIRST_CROSS:
                    step(1, -1, B + FIRST_CROSS[s])
            for s in range(0, B):
                step(1, 0, s)
            with eng.Fori(1, G - 1) as g:
                for b in range(B):
                    step(1, g, b)
            for s in range(STEPS - B, last):
                step(1, s // B, s % B)

        def refills(a, g):
            return not peeled(g) or (0 <= g < G and g + G * a + 1 < 2 * G)

        def early_keys(a, g, b):
            s = B * g + b
            return peeled(g) and (s in (0, 1) or s >= STEPS - 4 if a == 0 else s == STEPS - 2)

        def q_bank(g, b):
            early = {-4: B_P0, -3: B_Y, -2: B_O, -1: B_S, 0: B_O, 1: B_Y}
            return early.get(B * g + b, B_P0) if peeled(g) else B_P0

        def turn_banks(b):
            return (B_P0, B_P1) if b % 2 == 0 or b == 7 else (B_S, B_S + 1)

        def q_live(a, g, b):
            return live(g, b, 4 if a == 0 else 2)

        def q_block(g, b):
            return g + (b + 4) // B, (b + 4) // 4 % 2, b % 4

        block = top.enter_context(nc.Block())

        @block.sync
        def _(sp):
            def load_q(w, m, first=False):
                if not first:
                    sp.wait_ge(dve_wq if m < 2 else pool_wq, 2 * (w - 1) + m % 2 + 1)
                sp.dma_start(rawq[:, m], t["wq"][w, m]).then_inc(in_q[m], 16)

            def load_kv(w):
                need(sp, dve_wo, 2 * w)
                need(sp, pool_wo, 2 * w)
                sp.dma_start(rawko[:, 0:NC * 2 * HD], t["wkv"][w]).then_inc(in_kv, 16)

            def load_o(w):
                sp.wait_ge(dve_wkv, w + 1)
                sp.dma_start(rawko[:, :], t["wo"][w]).then_inc(in_o, 16)

            def load_bias(g):
                need(sp, dve_add, B * g)
                sp.dma_start(bias[:, :], t["bias"][g]).then_inc(in_bias, 16)

            load_q(0, 0, True)
            for i in range(2 * NC):
                n, c = i // NC, i % NC
                cols = slice(n * HALF, (n + 1) * HALF)
                sp.dma_start(xraw[:, c, cols], t["xT"][c][:, cols]).then_inc(in_x[i], 16)
                if i == NC - 1:
                    load_q(0, 1, True)
                    load_kv(0)
                    load_q(0, 2, True)
                    load_q(0, 3, True)
            load_bias(0)
            sp.wait_ge(dve_x, 2 * NC)
            sp.dma_start(acc[:, :, :], t["x"]).then_inc(in_acc, 16)
            sp.dma_start(qw[:, :], t["qw"]).then_inc(in_w, 16)
            sp.dma_start(kw[:, :], t["kw"]).then_inc(in_w, 16)

            def group(a, w, g, more):
                load_o(w)
                if more:
                    load_q(w + 1, 0)
                    load_q(w + 1, 1)
                    load_q(w + 1, 2)
                    load_q(w + 1, 3)
                    load_kv(w + 1)

            group(0, 0, 0, True)
            load_bias(1)
            with sp.Fori(1, G - 1) as g:
                group(0, g, g, True)
                load_bias(g + 1)
            def load_context(j):
                need(sp, pool_c, j - 1)
                sp.dma_start(rawc[:, j % 2], t["cT"][j // 2][:, (j % 2) * HALF:(j % 2 + 1) * HALF]).then_inc(in_c[j % 2], 16)
            load_context(0)
            load_context(1)
            load_o(G - 1)
            for m in range(HPG):
                load_q(G, m)
            load_context(2)
            load_context(3)
            load_kv(G)
            for j in range(4, 2 * NC):
                load_context(j)
            with sp.Fori(G, 2 * G - 1) as w:
                group(1, w, w, True)
            group(1, 2 * G - 1, G - 1, False)

            sp.wait_ge(kv_done[1], STEPS)
            for i in range(2):
                sp.dma_start(wraw[:, i], t["w13"][i]).then_inc(in_ff[i], 16)
            for i in range(2):
                sp.dma_start(braw[:, i], t["b13"][i]).then_inc(in_ff[3], 16)
            sp.dma_start(apad[:, :, :], t["apad"]).then_inc(in_ff[2], 16)
            for k in range(3):
                sp.dma_start(w2raw[0:KT[k], k, :], t["w2T"][128 * k:128 * k + KT[k], :]).then_inc(in_ff[6], 16)
            sp.wait_ge(sc_done[1], STEPS)
            sp.dma_start(b2raw[:, :], t["b2T"]).then_inc(in_ff[4], 16)
            sp.wait_ge(o_done[1], STEPS)
            sp.dma_start(a2raw[:, :, :], t["a2pad"]).then_inc(in_ff[5], 16)
            for b in range(B):
                sp.wait_ge(l3_ok, b + 1)
                sp.dma_start(t["out"][b], acc[:, b, :]).then_inc(out_ok, 16)
            sp.wait_ge(out_ok, 16 * B)

        @block.tensor
        def _(pe):
            def parts(lH, lL, rH, rL):
                return ((lH, rH), (lH, rL), (lL, rH))

            def project_q_heads(g, b):
                s2 = B * g + b + 2
                bb_ = (b + 2) % B
                if bb_ == 0:
                    pe.wait_ge(dve_wq, 2 * (g + (b + 2) // B + G + 1))
                    pe.wait_ge(pool_wq, 2 * (g + (b + 2) // B + G + 1))
                if peeled(g) and g < 0:
                    pe.wait_ge(dve_k[0], STEPS)
                    need(pe, act_q[1], s2)
                if peeled(g) and s2 < B:
                    pe.wait_ge(dve_lnt, s2 + 1)
                need(pe, dve_k[1], s2 - 1)
                tok = slice(bb_ * S, (bb_ + 1) * S)
                for c in range(NC):
                    for i, (l, r) in enumerate(parts(xH[:, c, tok], xL[:, c, tok], wqH[:, :, c, :], wqL[:, :, c, :])):
                        mm = pe.matmul(ps[:, B_P0, :], l, r, start=c == 0 and i == 0, stop=c == NC - 1 and i == 2)
                mm.then_inc(q_done[1], 1)

            def turn_q(g, b):
                s = B * g + b
                pe.wait_ge(act_qraw, s + 3)
                if peeled(g) and s == -2:
                    pe.wait_ge(dve_p[0], STEPS)
                if peeled(g) and s <= 0:
                    need(pe, dve_q[1], s + 2)
                for h in range(HPG):
                    mm = pe.transpose(ps[:, B_T, h * S:(h + 1) * S], qraw[:, h * HD:(h + 1) * HD], ident[:, :])
                mm.then_inc(qt_done, 1)

            def project_q(a, g, b):
                gq, half, m = q_block(g, b)
                n = B * g + b + 4
                s = B * g + b
                if half == 0:
                    pe.wait_ge(dve_wq if m < 2 else pool_wq, 2 * gq + m % 2 + 1)
                need(pe, dve_k[a], s + 1)
                if peeled(g) and n in (4, 5, 6):
                    pe.wait_ge(dve_q[0], {4: 3, 5: 2, 6: 1}[n])
                for c in range(NC):
                    if a == 0 and peeled(g) and n in (0, 4):
                        pe.wait_ge(dve_x, NC * half + c + 1)
                    for i, (l, r) in enumerate(parts(wqH[:, m, c], wqL[:, m, c], xH[:, c, half * HALF:(half + 1) * HALF],
                                                     xL[:, c, half * HALF:(half + 1) * HALF])):
                        mm = pe.matmul(ps[:, q_bank(g, b), :], l, r, start=c == 0 and i == 0, stop=c == NC - 1 and i == 2)
                mm.then_inc(q_done[a], 1)

            def project_kv(a, g, b, sources=None):
                s2 = B * g + b + 2
                bb_ = (b + 2) % B
                if sources != 1 and bb_ == 0:
                    pe.wait_ge(dve_wkv, g + (b + 2) // B + G * a + 1)
                if sources != 1:
                    need(pe, dve_v[a], s2)
                if a == 0 and peeled(g) and s2 == 0:
                    pe.wait_ge(dve_x, NC)
                if a == 1 and peeled(g) and s2 == 0:
                    pe.wait_ge(pool_c, 2 * NC)
                    pe.wait_ge(dve_v[0], STEPS)
                if a == 1 and peeled(g) and s2 < B and sources != 0:
                    pe.wait_ge(dve_lnt, s2 + 1)
                tiles = ((xH, xL),) if a == 0 else ((cH, cL), (xH, xL))
                for j, (sH, sL) in enumerate(tiles):
                    if sources in (None, j):
                        for c in range(NC):
                            tok = slice(bb_ * S, (bb_ + 1) * S)
                            for i, (l, r) in enumerate(parts(sH[:, c, tok], sL[:, c, tok], wkH[:, c, :], wkL[:, c, :])):
                                mm = pe.matmul(ps[:, B_P1, j * 2 * HD:(j + 1) * 2 * HD], l, r,
                                               start=c == 0 and i == 0, stop=c == NC - 1 and i == 2)
                if sources != 0:
                    mm.then_inc(kv_done[a], 1)

            def turn_keys(a, g, b):
                s1 = B * g + b + 1
                par = (b + 1) % 2
                if a == 0:
                    pe.wait_ge(act_kv[0], s1 + 1)
                else:
                    pe.wait_ge(pool_k, s1 + 1)
                if a == 1:
                    pe.wait_ge(act_q[1], s1 + 2 if live(g, b, 2) else STEPS)
                elif peeled(g) and s1 <= 2:
                    pe.wait_ge(dve_q[0], 1)
                else:
                    pe.wait_ge(dve_q[0], s1 + 4 if live(g, b, 4) else STEPS)
                for j in range(a + 1):
                    src = kraw[:, par, 0] if a == 0 else kn[:, j]
                    mm = pe.transpose(ps[:, B_P0, j * S:(j + 1) * S], src, ident[:, :])
                mm.then_inc(kt_done[a], 1)

            def scores(a, g, b):
                s = B * g + b
                half, tok = b // 4, slice((b % 4) * S, (b % 4 + 1) * S)
                if a == 1:
                    pe.wait_ge(dve_q[1], s + 1)
                    half, tok = b % 2, slice(0, S)
                elif b % 4 == 0:
                    pe.wait_ge(dve_q[0], s + 4)
                pe.wait_ge(dve_k[a], s + 1)
                need(pe, dve_add if a == 0 else act_exp[1], s)
                n = S * (a + 1)
                for h in range(HPG):
                    out = ps[:, B_S + h // 2, h % 2 * 256:h % 2 * 256 + 256]
                    if a == 0:
                        pe.matmul(out, QH[:, half, h, tok], KHL[:, b % 2, :, 0:n], start=True, stop=False,
                                  skip_group_check=True)
                        mm = pe.matmul(out[:, 0:n], QL[:, half, h, tok], KHL[:, b % 2, 0, 0:n], start=False, stop=True,
                                       skip_group_check=True)
                    else:
                        for i, (l, r) in enumerate(parts(QH[:, half, h, tok], QL[:, half, h, tok],
                                                         KHL[:, b % 2, 0], KHL[:, b % 2, 1])):
                            mm = pe.matmul(out, l, r, start=i == 0, stop=i == 2)
                mm.then_inc(sc_done[a], 1)

            def turn_probs(a, g, b):
                s = B * g + b
                pe.wait_ge(pool_p[a], s)
                if a == 1:
                    pe.wait_ge(dve_q[1], s + 2 if live(g, b, 1) else STEPS)
                if a == 1 and peeled(g) and s == 1:
                    pe.wait_ge(dve_lnt, B)
                for j in range(a + 1):
                    for h in range(HPG):
                        mm = pe.transpose(ps[:, B_T + j, h * S:(h + 1) * S], pr[:, h, j * S:(j + 1) * S], ident[:, :])
                mm.then_inc(pt_done[a], 1)

            def weigh_values(a, g, b):
                s = B * g + b
                if a == 0 and peeled(g) and s == 1:
                    pe.wait_ge(dve_q[0], 5)
                v = (b - 1) % 4
                pe.wait_ge(dve_v[a], s)
                need(pe, dve_o[a], s - 1)
                for j in range(a + 1):
                    pe.wait_ge(dve_p[a], (a + 1) * (s - 1) + j + 1)
                    for i, (l, r) in enumerate(parts(VH[:, v, j], VL[:, v, j], PH[j][:, :], PL[j][:, :])):
                        mm = pe.matmul(ps[:, B_O, :], l, r, start=j == 0 and i == 0, stop=j == a and i == 2)
                mm.then_inc(pv_done[a], 1)

            def project_out(a, g, b):
                s = B * g + b
                if a == 0 and peeled(g) and s == 2:
                    pe.wait_ge(dve_q[0], 6)
                par = b % 2
                pe.wait_ge(dve_o[a], s - 1)
                need(pe, dve_y[a], s - 2)
                for h in range(HPG):
                    if b == 2:
                        pe.wait_ge(dve_wo if h < 2 else pool_wo, 2 * (g + G * a) + h % 2 + 1)
                    tok = slice(h * S, (h + 1) * S)
                    for i, (l, r) in enumerate(parts(OH[:, par, tok], OL[:, par, tok], woH[:, h], woL[:, h])):
                        mm = pe.matmul(ps[:, B_Y, :], l, r, start=h == 0 and i == 0, stop=h == HPG - 1 and i == 2)
                mm.then_inc(o_done[a], 1)

            def turn_norm(b):
                pe.wait_ge(ln_ok[0], b + 1)
                need(pe, dve_lnt, b)
                for c in range(NC):
                    mm = pe.transpose(ps[:, B_T + 1, c * P:(c + 1) * P], acc[:, b, c * P:(c + 1) * P], ident[:, :])
                mm.then_inc(lnt_done, 1)

            def turn_x2(b):
                pe.wait_ge(ff_xs, b + 1)
                if b == 0:
                    pe.wait_ge(dve_k[1], STEPS)
                    pe.wait_ge(dve_v[1], STEPS)
                    pe.wait_ge(act_exp[1], STEPS)
                need(pe, ff_xsL, b - 1 if b < 7 else b)
                one, two = turn_banks(b)
                for c in range(NC):
                    pe.transpose(ps[:, one, c * P:(c + 1) * P], acc[:, b, c * P:(c + 1) * P], ident[:, :])
                pe.transpose(ps[:, two, 0:P], xs[:, b, :], ident[:, :]).then_inc(ff_t_done, 1)

            def lora_in(n):
                pe.wait_ge(in_ff[2], 16)
                pe.wait_ge(ff_x2T, B // 2 * (n + 1))
                pe.wait_ge(dve_o[1] if n == 0 else dve_y[1], STEPS)
                for c in range(NC):
                    mm = pe.matmul(ps[:, B_O + n, :], apad[:, c, :], x2T[:, c, n * HALF:(n + 1) * HALF],
                                   start=c == 0, stop=c == NC - 1)
                mm.then_inc(lora_done, 1)

            def step(a, g, b):
                s = B * g + b
                keys_first = early_keys(a, g, b)
                early_kv = peeled(g) and (s == -2 and a == 0 or -2 <= s < 2 and a == 1)
                last = peeled(g) and s >= STEPS - 4
                out_first = a == 1 and peeled(g) and s == STEPS
                if live(g, b, 0):
                    scores(a, g, b)
                if out_first:
                    project_out(a, g, b)
                if live(g, b, -1):
                    turn_probs(a, g, b)
                if early_kv and a == 0:
                    project_kv(a, g, b)
                if q_live(a, g, b):
                    if a == 0:
                        project_q(a, g, b)
                    else:
                        project_q_heads(g, b)
                if early_kv and a == 1:
                    project_kv(a, g, b, 0)
                if a == 1 and peeled(g):
                    for c in FF_EARLY.get(s, ()):
                        turn_x2(c)
                if a == 0 and peeled(g) and s >= STEPS - 4:
                    turn_norm(s - (STEPS - 4))
                if keys_first and live(g, b, 1):
                    turn_keys(a, g, b)
                if last and not out_first and live(g, b, -2):
                    project_out(a, g, b)
                if live(g, b, -1):
                    weigh_values(a, g, b)
                if not last and live(g, b, -2):
                    project_out(a, g, b)
                if a == 1 and peeled(g):
                    for c in FF_LATE.get(s, ()):
                        turn_x2(c)
                if a == 1 and live(g, b, 2):
                    turn_q(g, b)
                if not keys_first and live(g, b, 1):
                    turn_keys(a, g, b)
                if early_kv and a == 1:
                    project_kv(a, g, b, 1)
                if live(g, b, 2) and not early_kv:
                    project_kv(a, g, b)

            pe.wait_ge(id_ok, 1)
            for i in range(WARM_UP):
                pe.transpose(ps[:, B_P1, i % 4 * P:(i % 4 + 1) * P], ident[:, :], ident[:, :])
            steps(pe, step, STEPS + 2)

            lora_in(0)

            def lora2(u):
                n, k = u // NT, u % NT
                rows = KT[k % 3]
                pe.wait_ge(ff_midL, u + 1)
                if u == 0:
                    pe.wait_ge(ff_a2L, 1)
                for i, (l, r) in enumerate(((a2A, midH), (a2B, midL))):
                    x = pe.matmul(ps[:, B_O + n, :], l[0:rows, k, :], r[0:rows, u % 2, :],
                                  start=k == 0 and i == 0, stop=k == NT - 1 and i == 1, skip_group_check=True)
                x.then_inc(lora2_done, 1)

            for n in range(2):
                pe.wait_ge(ff_xsL, 6 if n == 0 else B)
                for k in range(NT):
                    u = n * NT + k
                    rows = KT[k % 3]
                    cols = slice(k * P, k * P + rows)
                    tok = slice(n * HALF, (n + 1) * HALF)
                    need(pe, ff_mid, u - 1)
                    for i in range(2):
                        if u == 0:
                            pe.wait_ge(ff_wL[i], 1)
                        out = ps[0:rows, 2 * (u % 2) + i, :]
                        for j, (l, r) in enumerate(parts(wgH[:, i, cols], wgL[:, i, cols], xsH[:, tok], xsL[:, tok])):
                            pe.matmul(out, l, r, start=j == 0, stop=False)
                        if k == 0 and i == 0:
                            pe.wait_ge(ff_ttL, n + 1)
                        if u == 0:
                            pe.wait_ge(ff_bL, i + 1)
                        mm = pe.matmul(out, bb[:, i, cols], tt[:, tok], start=False, stop=True)
                    mm.then_inc(up_done, 1)
                    if u >= 2:
                        lora2(u - 2)
                    if u in FF_TURN:
                        turn_x2(FF_TURN[u])
                    if u == FF_LORA:
                        lora_in(1)
            pe.wait_ge(ff_w2L, 3)
            pe.wait_ge(ff_b2L, 1)
            for b in range(B):
                if b == 1:
                    lora2(2 * NT - 2)
                    lora2(2 * NT - 1)
                tok = slice(b * S, (b + 1) * S)
                if b % 4 == 0:
                    pe.wait_ge(ff_hsL, 3 * (b // 4 + 1))
                    pe.wait_ge(ff_tt2L, b // 4 + 1)
                need(pe, ff_y, b - 1)
                for k in range(3):
                    rows = KT[k]
                    for i, (l, r) in enumerate(parts(hsH[0:rows, k, tok], hsL[0:rows, k, tok],
                                                     w2H[0:rows, k], w2L[0:rows, k])):
                        pe.matmul(ps[:, 6 + b % 2, :], l, r, start=k == 0 and i == 0, stop=False)
                pe.matmul(ps[:, 6 + b % 2, :], tt2[:, tok], bb2[:, :], start=False, stop=True).then_inc(down_done, 1)

        @block.scalar
        def _(act):
            def high(out, src, scale=1.0):
                return act.activation(out, src, ACT.Copy, scale=scale)

            def split_wq(w, m):
                act.wait_ge(in_q[m], 16 * (w + 1))
                high(wqH[:, m], rawq[:, m]).then_inc(act_wq, 1)

            def split_wkv(w):
                act.wait_ge(in_kv, 16 * (w + 1))
                high(wkH[:, :, :], rawko[:, 0:NC * 2 * HD].rearrange("p (c n) -> p c n", c=NC)).then_inc(act_wkv, 1)

            def split_wo(w):
                act.wait_ge(in_o, 16 * (w + 1))
                for h in range(HPG):
                    high(woH[:, h], rawko[:, h * D:(h + 1) * D]).then_inc(act_wo, 1)

            def take_x2(b):
                one, two = turn_banks(b)
                act.wait_ge(ff_t_done, b + 1)
                act.activation(x2T[:, :, b * S:(b + 1) * S], ps[:, one, :].rearrange("p (c n) -> p c n", c=NC),
                               ACT.Copy).then_inc(ff_x2T, 1)
                high(xsH[:, b * S:(b + 1) * S], ps[:, two, 0:P]).then_inc(ff_xsH, 1)

            def high_keys(a, g, b):
                act.wait_ge(kt_done[a], B * g + b + 2)
                n, par = S * (a + 1), (b + 1) % 2
                high(KHL[:, par, 0, 0:n], ps[:, B_P0, 0:n], 1.0 if a == 0 else qkw[:, 0:1]).then_inc(act_k[a], 1)

            def step(a, g, b):
                s = B * g + b
                w = g + G * a
                refill = refills(a, g)
                if a == 1 and peeled(g) and s == -1:
                    act.wait_ge(qkw_ok, 1)
                if live(g, b, 1):
                    act.wait_ge(kv_done[a], s + 2)
                    kv = ps[:, B_P1, 0:(a + 1) * 2 * HD].rearrange("p (j n) -> p j n", n=2 * HD)
                    v, par = (b + 1) % 4, (b + 1) % 2
                    high(VH[:, v, 0:a + 1], kv[:, :, HD:2 * HD])
                    if a == 0:
                        act.activation(kraw[:, par, 0:1], kv[:, :, 0:HD], ACT.Copy).then_inc(act_kv[0], 1)
                    else:
                        act.activation(kraw[:, par, 0:2], kv[:, :, 0:HD], ACT.Copy)
                        for j in range(2):
                            x = act.activation(junk[:, j], kv[:, j, 0:HD], ACT.Square, scale=SCALE, accum_out=kss[:, par, j:j + 1])
                        x.then_inc(act_kv[1], 1)
                if b == 6 and refill and not early_keys(a, g, b):
                    split_wkv(w + 1)
                if live(g, b, -1):
                    act.wait_ge(pt_done[a], s)
                    for j in range(a + 1):
                        high(PH[j][:, :], ps[:, B_T + j, :]).then_inc(act_p[a], 1)
                if early_keys(a, g, b) and live(g, b, 1):
                    high_keys(a, g, b)
                if a == 1 and peeled(g):
                    for c in FF_EARLY.get(s, ()):
                        take_x2(c)
                if a == 0 and b == 2 and live(g, b, 0):
                    need(act, o_done[0], s - 2)
                    split_wo(w)
                if live(g, b, 0):
                    act.wait_ge(dve_max[a], s + 1)
                    for h in range(HPG):
                        if a == 0:
                            x = act.activation(pr[:, h, 0:S], sc_b[:, h * S:(h + 1) * S], ACT.Exp,
                                               bias=nmax[:, h:h + 1], accum_out=sums[:, h:h + 1])
                        else:
                            x = act.activation(pr[:, h, :], ps[:, B_S + h // 2, (h % 2) * 256:(h % 2 + 1) * 256], ACT.Exp,
                                               bias=nbias[:, h:h + 1], scale=qsc[:, b % 2, h:h + 1],
                                               accum_out=sums[:, h:h + 1])
                    x.then_inc(act_exp[a], 1)
                if a == 0 and q_live(a, g, b):
                    _, half, m = q_block(g, b)
                    act.wait_ge(q_done[0], s + 5)
                    high(QH[:, half, m], ps[:, q_bank(g, b), :], SCALE).then_inc(act_q[0], 1)
                if a == 1 and q_live(a, g, b):
                    act.wait_ge(q_done[1], s + 3)
                    need(act, qt_done, s + 2)
                    act.activation(qraw[:, :], ps[:, B_P0, :], ACT.Copy).then_inc(act_qraw, 1)
                    need(act, dve_qms, s + 2)
                    act.wait_ge(act_qraw, s + 3)
                    for h in range(HPG):
                        head = ps[:, B_P0, h * HD:(h + 1) * HD]
                        x = act.activation(head, head, ACT.Square, accum_out=qss[:, h:h + 1])
                    x.then_inc(act_q[1], 1)
                if a == 0 and peeled(g) and s >= STEPS - 4:
                    c = s - (STEPS - 4)
                    act.wait_ge(lnt_done, c + 1)
                    high(xH[:, :, c * S:(c + 1) * S], ps[:, B_T + 1, :].rearrange("p (c n) -> p c n", c=NC)).then_inc(act_lnt, 1)
                if live(g, b, -1):
                    act.wait_ge(pv_done[a], s)
                    need(act, o_done[a], s - 2)
                    high(OH[:, (b - 1) % 2], ps[:, B_O, :]).then_inc(act_o[a], 1)
                if a == 1 and q_live(a, g, b):
                    act.wait_ge(qt_done, s + 3)
                    high(QH[:, b % 2, :, 0:S], ps[:, B_T, :].rearrange("p (h n) -> p h n", h=HPG)).then_inc(act_qt, 1)
                if a == 1 and peeled(g):
                    for c in FF_LATE.get(s, ()):
                        take_x2(c)
                    if s in (STEPS - 1, STEPS):
                        i = s - (STEPS - 1)
                        act.wait_ge(in_ff[i], 16)
                        high(wgH[:, i], wraw[:, i]).then_inc(ff_wH, 1)
                        act.wait_ge(in_ff[3], 16 * 2)
                        high(bb[:, i], braw[:, i]).then_inc(ff_bH, 1)
                if a == 0 and b < 4 and refill:
                    split_wq(w + 1, b)
                if not early_keys(a, g, b) and live(g, b, 1):
                    high_keys(a, g, b)
                if a == 0 and peeled(g) and s == STEPS:
                    split_wkv(G)
                if a == 1 and b == 1 and live(g, b, 0):
                    need(act, o_done[1], s - 1)
                    if peeled(g) and g == 0:
                        act.wait_ge(o_done[0], STEPS)
                    split_wo(w)
                if a == 1 and b == 5 and refill:
                    for m in WQ_ORDER:
                        split_wq(w + 1, m)
                if a == 0 and peeled(g) and g == G - 1:
                    act.wait_ge(in_c[b % 2], 16 * (b // 2 + 1))
                    high(cH[:, b // 2, (b % 2) * HALF:(b % 2 + 1) * HALF], rawc[:, b % 2]).then_inc(act_c, 1)

            split_wq(0, 0)
            def split_x(n):
                for c in range(NC):
                    cols = slice(n * HALF, (n + 1) * HALF)
                    act.wait_ge(in_x[n * NC + c], 16)
                    high(xH[:, c, cols], xraw[:, c, cols]).then_inc(act_x, 1)

            split_x(0)
            split_wq(0, 1)
            split_wkv(0)
            split_wq(0, 2)
            split_wq(0, 3)
            split_x(1)
            steps(act, step, STEPS + 2)

            def lora_high(n):
                act.wait_ge(lora_done, n + 1)
                high(tt[:, n * HALF:(n + 1) * HALF], ps[:, B_O + n, :], LORA).then_inc(ff_ttH, 1)

            def split_mid(u):
                rows = KT[u % NT % 3]
                act.wait_ge(ff_mid, u + 1)
                need(act, lora2_done, u - 1)
                high(midH[0:rows, u % 2], mid[0:rows, u % 3]).then_inc(ff_midH, 1)

            def finish_sum(n, k):
                act.wait_ge(ff_hs, n * NT + 9 + k + 1)
                high(hsH[0:KT[k], k, n * HALF:(n + 1) * HALF], hs[0:KT[k], k, :]).then_inc(ff_hsH, 1)

            def finish_t2(n):
                cols = slice(n * HALF, (n + 1) * HALF)
                act.wait_ge(lora2_done, NT * (n + 1))
                high(tt2[:, cols], ps[:, B_O + n, :], LORA).then_inc(ff_tt2H, 1)

            act.wait_ge(in_ff[5], 16)
            high(a2A[:, :, :], a2raw[:, :, :])
            lora_high(0)
            for n in range(2):
                for k in range(NT):
                    u = n * NT + k
                    rows = KT[k % 3]
                    act.wait_ge(up_done, u + 1)
                    need(act, ff_mid, u - 1)
                    act.activation(gate[0:rows, u % 2], ps[0:rows, 2 * (u % 2), :], ACT.Silu).then_inc(ff_gate, 1)
                    if u == 0:
                        act.wait_ge(zero_a2, 1)
                        wide = [v[:, :, :].rearrange("p k (q c) -> p k q c", q=4) for v in (a2B, a2raw)]
                        for q in range(4):
                            x = high(wide[0][:, :, q, 0:2], wide[1][:, :, q, 0:2])
                        x.then_inc(ff_a2H, 1)
                    if u >= 1:
                        split_mid(u - 1)
                    if u in FF_TURN:
                        take_x2(FF_TURN[u])
                    if u == FF_LORA:
                        lora_high(1)
                    if 7 <= u < 10:
                        j = u - 7
                        act.wait_ge(in_ff[6], 16 * 3)
                        high(w2H[0:KT[j], j], w2raw[0:KT[j], j]).then_inc(ff_w2H, 1)
                    if u == 10:
                        act.wait_ge(in_ff[4], 16)
                        high(bb2[:, :], b2raw[:, :]).then_inc(ff_b2H, 1)
                    if NT <= u < NT + 3:
                        finish_sum(0, u - NT)
                    if u == NT + 3:
                        finish_t2(0)
            split_mid(2 * NT - 1)
            for k in range(3):
                finish_sum(1, k)
            finish_t2(1)

        @block.vector
        def _(dve):
            def low(out, src, hi):
                return dve.tensor_tensor(out, src, f32(hi), ALU.subtract)

            def split_wkv(w):
                dve.wait_ge(act_wkv, w + 1)
                low(wkL[:, :, :], rawko[:, 0:NC * 2 * HD].rearrange("p (c n) -> p c n", c=NC), wkH[:, :, :]).then_inc(dve_wkv, 1)

            def norm_stats(a, b):
                dve.wait_ge(dve_y[a], STEPS - B + b + 1)
                dve.bn_stats(bn6[:, b, :], acc[:, b, :]).then_inc(ln_bn[a], 1)
                dve.wait_ge(ln_bn[a], b + 1)
                dve.bn_aggr(mv[:, b, :], bn6[:, b, :]).then_inc(ln_mv[a], 1)
                dve.wait_ge(ln_mv[a], b + 1)
                dve.tensor_scalar(ve[:, b:b + 1], mv[:, b, 1:2], LN_EPS, None, ALU.add).then_inc(ln_ve[a], 1)

            def norm_apply(a, b):
                dve.wait_ge(ln_rs[a], b + 1)
                dve.tensor_scalar(acc[:, b, :], acc[:, b, :], mv[:, b, 0:1], rstd[:, b:b + 1],
                                  ALU.subtract, ALU.mult).then_inc(ln_ok[a], 1)

            def take_xs(b):
                dve.wait_ge(ff_xsH, b + 1)
                low(xsL[:, b * S:(b + 1) * S], ps[:, turn_banks(b)[1], 0:P], xsH[:, b * S:(b + 1) * S]).then_inc(ff_xsL, 1)

            def split_wq(w, m, at=None):
                dve.wait_ge(act_wq, HPG * w + (m if at is None else at) + 1)
                low(wqL[:, m], rawq[:, m], wqH[:, m]).then_inc(dve_wq, 1)

            def lora_low(n, out, hi_done, lo_done):
                dve.wait_ge(hi_done, n + 1)
                cols = slice(n * HALF, (n + 1) * HALF)
                dve.scalar_tensor_tensor(out=out[64:128, cols], in0=ps[64:128, B_O + n, :], scalar=LORA,
                                         in1=f32(out[64:128, cols]), op0=ALU.mult, op1=ALU.subtract).then_inc(lo_done, 1)

            def split_wo(w):
                for h in (0, 1):
                    dve.wait_ge(act_wo, HPG * w + h + 1)
                    low(woL[:, h], rawko[:, h * D:(h + 1) * D], woH[:, h]).then_inc(dve_wo, 1)

            def low_up():
                dve.wait_ge(ff_wH, 1)
                low(wgL[:, 0], wraw[:, 0], wgH[:, 0]).then_inc(ff_wL[0], 1)

            def by_rows(out, src):
                return dve.scalar_tensor_tensor(out=out, in0=f32(out), scalar=lows[:, 0:1], in1=src, op0=ALU.mult, op1=ALU.add)

            def low_up_b(i):
                dve.wait_ge(ff_bH, i + 1)
                by_rows(bb[:, i], braw[:, i]).then_inc(ff_bL, 1)

            def residual(a, g, b):
                s = B * g + b
                if a == 0 and peeled(g) and s == 2:
                    dve.wait_ge(in_acc, 16)
                dve.wait_ge(o_done[a], s - 1)
                need(dve, dve_y[a], s - 2)
                bb_ = (b - 2) % B
                dve.tensor_tensor(acc[:, bb_, :], ps[:, B_Y, :], acc[:, bb_, :], ALU.add).then_inc(dve_y[a], 1)

            def inverse_sums(a, s):
                dve.wait_ge(act_exp[a], s + 1)
                need(dve, pool_p[a], s)
                dve.reciprocal(rsum[:, :], sums[:, :]).then_inc(dve_rs[a], 1)

            def low_probs(a, g, b):
                for j in range(a + 1):
                    dve.wait_ge(act_p[a], (a + 1) * (B * g + b - 1) + j + 1)
                    low(PL[j][:, :], ps[:, B_T + j, :], PH[j][:, :]).then_inc(dve_p[a], 1)

            def low_keys(a, g, b):
                dve.wait_ge(act_k[a], B * g + b + 2)
                n, par = S * (a + 1), (b + 1) % 2
                if a == 0:
                    low(KHL[:, par, 1, 0:n], ps[:, B_P0, 0:n], KHL[:, par, 0, 0:n]).then_inc(dve_k[0], 1)
                else:
                    dve.scalar_tensor_tensor(out=KHL[:, par, 1, 0:n], in0=ps[:, B_P0, 0:n], scalar=qkw[:, 0:1],
                                             in1=f32(KHL[:, par, 0, 0:n]), op0=ALU.mult, op1=ALU.subtract).then_inc(dve_k[1], 1)

            def step(a, g, b):
                s = B * g + b
                w = g + G * a
                if a == 1 and peeled(g) and s == -2:
                    dve.wait_ge(in_w, 32)
                    dve.tensor_tensor(qkw[:, :], qw[:, :], kw[:, :], ALU.mult).then_inc(qkw_ok, 1)
                if a == 1 and peeled(g) and s == -1:
                    dve.wait_ge(qkw_ok, 1)
                refill = refills(a, g)
                keys_before_sum = peeled(g) and s >= STEPS - 6
                sum_early = peeled(g) and (STEPS - 4 <= s < STEPS if a == 0 else s in (STEPS - 1, STEPS))
                stats_held = a == 0 and peeled(g) and STEPS - 4 <= s < STEPS
                held_before = a == 0 and peeled(g) and STEPS - 4 < s <= STEPS
                softmax_held = held_before and s < STEPS
                if live(g, b, 1):
                    dve.wait_ge(act_kv[a], s + 2)
                    kv = ps[:, B_P1, 0:(a + 1) * 2 * HD].rearrange("p (j n) -> p j n", n=2 * HD)
                    v = (b + 1) % 4
                    low(VL[:, v, 0:a + 1], kv[:, :, HD:2 * HD], VH[:, v, 0:a + 1]).then_inc(dve_v[a], 1)
                if live(g, b, 0):
                    dve.wait_ge(sc_done[a], s + 1)
                    if a == 0:
                        if b == 0:
                            dve.wait_ge(in_bias, 16 * (g + 1))
                        need(dve, act_exp[0], s)
                        both = ps[:, B_S:B_S + 2, :].rearrange("p j (h i k) -> p (j h) i k", h=2, i=2)
                        shaped = [v[:, :].rearrange("p (h k) -> p h k", h=HPG) for v in (sc_b, bias)]
                        dve.tensor_tensor(shaped[0], both[:, :, 1], shaped[1], ALU.add).then_inc(dve_bias, 1)
                        dve.wait_ge(dve_bias, s + 1)
                        dve.tensor_tensor(shaped[0], both[:, :, 0], shaped[0], ALU.add).then_inc(dve_add, 1)
                        if not softmax_held and live(g, b, -1):
                            low_probs(a, g, b)
                        dve.wait_ge(dve_add, s + 1)
                        dve.tensor_reduce(nmax[:, :], sc_b[:, :].rearrange("p (h k) -> p h k", h=HPG), AX.X, ALU.max,
                                          negate=True).then_inc(dve_max[0], 1)
                    else:
                        dve.tensor_reduce(nmax[:, :], ps[:, B_S:B_S + 2, :].rearrange("p j (h k) -> p (j h) k", h=2),
                                          AX.X, ALU.max, negate=True).then_inc(dve_nm, 1)
                        dve.wait_ge(dve_nm, s + 1)
                        dve.wait_ge(pool_q, s + 1)
                        need(dve, act_exp[1], s)
                        dve.tensor_tensor(nbias[:, :], nmax[:, :], qsc[:, b % 2, :], ALU.mult).then_inc(dve_max[1], 1)
                if early_keys(a, g, b) and live(g, b, 1):
                    low_keys(a, g, b)
                if live(g, b, -1) and (a == 1 or softmax_held or not live(g, b, 0)):
                    low_probs(a, g, b)
                if held_before:
                    norm_stats(a, s - 3 - (STEPS - B))
                if softmax_held:
                    inverse_sums(a, s)
                if a == 1 and peeled(g):
                    for c in FF_EARLY.get(s, ()):
                        take_xs(c)
                    if sum_early:
                        residual(a, g, b)
                    if s == STEPS + 1:
                        low_up_b(1)
                if b == 6 and refill and not early_keys(a, g, b):
                    split_wkv(w + 1)
                if peeled(g) and s - 3 >= STEPS - B and live(g, b, -3):
                    norm_apply(a, s - 3 - (STEPS - B))
                if a == 0 and b == 2 and live(g, b, 0):
                    split_wo(w)
                if live(g, b, 0) and not softmax_held:
                    inverse_sums(a, s)
                if a == 0 and sum_early:
                    residual(a, g, b)
                if a == 0 and q_live(a, g, b):
                    _, half, m = q_block(g, b)
                    dve.wait_ge(act_q[0], s + 5)
                    dve.scalar_tensor_tensor(out=QL[:, half, m], in0=ps[:, q_bank(g, b), :], scalar=SCALE,
                                             in1=f32(QH[:, half, m]), op0=ALU.mult, op1=ALU.subtract).then_inc(dve_q[0], 1)
                if a == 0 and peeled(g) and s >= STEPS - 4:
                    c = s - (STEPS - 4)
                    dve.wait_ge(act_lnt, c + 1)
                    low(xL[:, :, c * S:(c + 1) * S], ps[:, B_T + 1, :].rearrange("p (c n) -> p c n", c=NC),
                        xH[:, :, c * S:(c + 1) * S]).then_inc(dve_lnt, 1)
                if live(g, b, -1):
                    dve.wait_ge(act_o[a], s)
                    low(OL[:, (b - 1) % 2], ps[:, B_O, :], OH[:, (b - 1) % 2]).then_inc(dve_o[a], 1)
                if a == 1 and q_live(a, g, b):
                    dve.wait_ge(act_q[1], s + 3)
                    need(dve, pool_q, s + 2)
                    dve.tensor_scalar(qms[:, :], qss[:, :], HD * RMS_EPS, None, ALU.add).then_inc(dve_qms, 1)
                    dve.wait_ge(act_qt, s + 3)
                    low(QL[:, b % 2, :, 0:S], ps[:, B_T, :].rearrange("p (h n) -> p h n", h=HPG),
                        QH[:, b % 2, :, 0:S]).then_inc(dve_q[1], 1)
                if a == 1 and peeled(g):
                    for c in FF_LATE.get(s, ()):
                        take_xs(c)
                    for c in FF_XS.get(s, ()):
                        dve.wait_ge(ln_ok[1], c + 1)
                        dve.tensor_reduce(xs[:, c, :], acc[:, c, :].rearrange("p (c f) -> p f c", c=NC), AX.X,
                                          ALU.add).then_inc(ff_xs, 1)
                    if s == STEPS + 1:
                        lora_low(0, tt, ff_ttH, ff_ttL)
                if keys_before_sum and not early_keys(a, g, b) and live(g, b, 1):
                    low_keys(a, g, b)
                if live(g, b, -2) and not sum_early:
                    residual(a, g, b)
                if peeled(g) and s - 2 >= STEPS - B and live(g, b, -2) and not stats_held:
                    norm_stats(a, s - 2 - (STEPS - B))
                if a == 0 and peeled(g) and s == STEPS:
                    split_wkv(G)
                if a == 1 and peeled(g) and s == STEPS - 1:
                    low_up()
                if a == 1 and peeled(g) and s == STEPS:
                    low_up_b(0)
                if not keys_before_sum and not early_keys(a, g, b) and live(g, b, 1):
                    low_keys(a, g, b)
                if a == 0 and b < 2 and refill:
                    split_wq(w + 1, b)
                if a == 1 and b == 1 and live(g, b, 0):
                    split_wo(w)
                if a == 1 and b == 5 and refill:
                    for m in (0, 1):
                        split_wq(w + 1, m, WQ_ORDER.index(m))

            def split_x(n):
                for c in range(NC):
                    cols = slice(n * HALF, (n + 1) * HALF)
                    dve.wait_ge(act_x, n * NC + c + 1)
                    low(xL[:, c, cols], xraw[:, c, cols], xH[:, c, cols]).then_inc(dve_x, 1)

            for q in range(4):
                dve.memset(lows[32 * q:32 * q + 32, :], -float(q % 2)).then_inc(lows_ok, 1)
            split_wq(0, 0)
            split_x(0)
            split_wq(0, 1)
            split_wkv(0)
            split_x(1)
            dve.wait_ge(lows_ok, 4)
            steps(dve, step, STEPS + 3)

            def split_mid(u):
                rows = KT[u % NT % 3]
                dve.wait_ge(ff_midH, u + 1)
                low(midL[0:rows, u % 2], mid[0:rows, u % 3], midH[0:rows, u % 2]).then_inc(ff_midL, 1)

            def finish_sum(n, k):
                cols = slice(n * HALF, (n + 1) * HALF)
                dve.wait_ge(ff_hsH, n * 3 + k + 1)
                low(hsL[0:KT[k], k, cols], hs[0:KT[k], k, :], hsH[0:KT[k], k, cols]).then_inc(ff_hsL, 1)

            for n in range(2):
                for k in range(NT):
                    u = n * NT + k
                    rows = KT[k % 3]
                    dve.wait_ge(ff_gate, u + 1)
                    need(dve, ff_hs, u - 2)
                    need(dve, ff_midL, u - 2)
                    dve.tensor_tensor(mid[0:rows, u % 3], ps[0:rows, 2 * (u % 2) + 1, :], gate[0:rows, u % 2],
                                      ALU.mult).then_inc(ff_mid, 1)
                    if u == 0:
                        dve.wait_ge(ff_a2H, 1)
                        wide = [v[:, :, :].rearrange("p k (q c) -> p k q c", q=4) for v in (a2A, a2raw)]
                        for q in range(4):
                            x = low(wide[0][:, :, q, 2:4], wide[1][:, :, q, 2:4], wide[0][:, :, q, 2:4])
                        x.then_inc(ff_a2L, 1)
                    if u >= 1:
                        split_mid(u - 1)
                    if u in FF_TURN:
                        take_xs(FF_TURN[u])
                    if u == FF_LORA:
                        lora_low(1, tt, ff_ttH, ff_ttL)
                    if 7 <= u < 10:
                        j = u - 7
                        dve.wait_ge(ff_w2H, j + 1)
                        low(w2L[0:KT[j], j], w2raw[0:KT[j], j], w2H[0:KT[j], j]).then_inc(ff_w2L, 1)
                    if u == 10:
                        dve.wait_ge(ff_b2H, 1)
                        by_rows(bb2[:, :], b2raw[:, :]).then_inc(ff_b2L, 1)
                    if NT <= u < NT + 3:
                        finish_sum(0, u - NT)
                    if u == NT + 3:
                        lora_low(0, tt2, ff_tt2H, ff_tt2L)
            split_mid(2 * NT - 1)
            for b in range(B + 1):
                if b == 1:
                    for k in range(3):
                        finish_sum(1, k)
                    lora_low(1, tt2, ff_tt2H, ff_tt2L)
                if b < B:
                    dve.wait_ge(down_done, b + 1)
                    dve.tensor_tensor(acc[:, b, :], ps[:, 6 + b % 2, :], acc[:, b, :], ALU.add).then_inc(ff_y, 1)
                    dve.wait_ge(ff_y, b + 1)
                    dve.bn_stats(bn6[:, b, :], acc[:, b, :]).then_inc(l3_bn, 1)
                    dve.wait_ge(l3_bn, b + 1)
                    dve.bn_aggr(mv[:, b, :], bn6[:, b, :]).then_inc(l3_mv, 1)
                    dve.wait_ge(l3_mv, b + 1)
                    dve.tensor_scalar(ve[:, b:b + 1], mv[:, b, 1:2], LN_EPS, None, ALU.add).then_inc(l3_ve, 1)
                if b >= 1:
                    c = b - 1
                    dve.wait_ge(l3_rs, c + 1)
                    dve.tensor_scalar(acc[:, c, :], acc[:, c, :], mv[:, c, 0:1], rstd[:, c:c + 1],
                                      ALU.subtract, ALU.mult).then_inc(l3_ok, 1)

        @block.gpsimd
        def _(pool):
            def low(out, src, hi):
                return pool.tensor_tensor(out, src, f32(hi), ALU.subtract)

            def split_wq(w, m, at=None):
                pool.wait_ge(act_wq, HPG * w + (m if at is None else at) + 1)
                low(wqL[:, m], rawq[:, m], wqH[:, m]).then_inc(pool_wq, 1)

            def split_wo(w):
                for h in (2, 3):
                    pool.wait_ge(act_wo, HPG * w + h + 1)
                    low(woL[:, h], rawko[:, h * D:(h + 1) * D], woH[:, h]).then_inc(pool_wo, 1)

            def step(a, g, b):
                s = B * g + b
                w = g + G * a
                if a == 0 and b == 2 and live(g, b, 0):
                    split_wo(w)
                if a == 1 and live(g, b, 1):
                    par = (b + 1) % 2
                    pool.wait_ge(act_kv[1], s + 2)
                    pool.tensor_tensor(kms[:, :], kss[:, par, :], eps[:, :], ALU.add).then_inc(pool_kms, 1)
                    pool.wait_ge(pool_kms, s + 2)
                    pool.tensor_tensor(krs[:, :], kms[:, :], mhalf[:, 0:2], ALU.pow).then_inc(pool_krs, 1)
                    pool.wait_ge(pool_krs, s + 2)
                    need(pool, kt_done[1], s + 1)
                    pool.tensor_tensor(kn[:, :, :], kraw[:, par], krs[:, :].unsqueeze(2).to_broadcast([P, 2, HD]),
                                       ALU.mult).then_inc(pool_k, 1)
                if live(g, b, 0):
                    pool.wait_ge(dve_rs[a], s + 1)
                    n = S * (a + 1)
                    pool.tensor_tensor(pr[:, 0, 0:n], pr[:, 0, 0:n], rsum[:, 0:1].to_broadcast([P, n]), ALU.mult)
                    for h in range(1, HPG):
                        x = pool.tensor_scalar(pr[:, h, 0:n], pr[:, h, 0:n], rsum[:, h:h + 1], 1.0, ALU.mult, ALU.mult)
                    x.then_inc(pool_p[a], 1)
                refill = refills(a, g)
                if a == 0 and b in (2, 3) and refill:
                    split_wq(w + 1, b)
                if a == 0 and peeled(g) and g == G - 1:
                    pool.wait_ge(act_c, b + 1)
                    cols = slice((b % 2) * HALF, (b % 2 + 1) * HALF)
                    low(cL[:, b // 2, cols], rawc[:, b % 2], cH[:, b // 2, cols]).then_inc(pool_c, 1)
                if a == 1 and q_live(a, g, b):
                    pool.wait_ge(dve_qms, s + 3)
                    pool.tensor_tensor(qsc[:, b % 2, :], qms[:, :], mhalf[:, :], ALU.pow).then_inc(pool_q, 1)
                if a == 1 and b == 1 and live(g, b, 0):
                    split_wo(w)
                if a == 1 and b == 5 and refill:
                    for m in (2, 3):
                        split_wq(w + 1, m, WQ_ORDER.index(m))
                if peeled(g) and s - 2 >= STEPS - B and live(g, b, -2):
                    c = s - 2 - (STEPS - B)
                    pool.wait_ge(ln_ve[a], c + 1)
                    pool.tensor_tensor(rstd[:, c:c + 1], ve[:, c:c + 1], mhalf[:, 0:1], ALU.pow).then_inc(ln_rs[a], 1)
                if a == 1 and peeled(g) and s == STEPS:
                    pool.wait_ge(ff_wH, 2)
                    low(wgL[:, 1], wraw[:, 1], wgH[:, 1]).then_inc(ff_wL[1], 1)

            pool.memset(ident[:, :], 0.0).then_inc(z_id, 1)
            pool.wait_ge(z_id, 1)
            pool.affine_select(out=ident[:, :], in_=ident[:, :], compare_op=ALU.not_equal, fill=1.0, base=0,
                               pattern=[[-1, P]], channel_multiplier=1).then_inc(id_ok, 1)
            pool.memset(eps[:, :], RMS_EPS)
            pool.memset(mhalf[:, :], -0.5).then_inc(half_ok, 1)
            pool.wait_ge(half_ok, 1)
            for m in range(2, HPG):
                split_wq(0, m)
            steps(pool, step, STEPS + 2)

            pool.wait_ge(o_done[1], STEPS)
            pool.memset(f32(a2B[:, :, :]), 0.0).then_inc(zero_a2, 1)
            for n in range(2):
                for k in range(NT):
                    u = n * NT + k
                    rows = KT[k % 3]
                    pool.wait_ge(ff_mid, u + 1)
                    src = mid[0:rows, u % 3]
                    out = hs[0:rows, k % 3]
                    if k < 3:
                        if n == 1:
                            pool.wait_ge(ff_hsL, k + 1)
                        pool.tensor_copy(out, src).then_inc(ff_hs, 1)
                    else:
                        pool.wait_ge(ff_hs, u - 2)
                        pool.tensor_tensor(out, out, src, ALU.add).then_inc(ff_hs, 1)
            for b in range(B):
                pool.wait_ge(l3_ve, b + 1)
                pool.tensor_tensor(rstd[:, b:b + 1], ve[:, b:b + 1], mhalf[:, 0:1], ALU.pow).then_inc(l3_rs, 1)


def kernel(x, ctx_4096, L0_attn_w_qkv, L0_attn_w_o, L0_xattn_Wq, L0_xattn_Wk, L0_xattn_Wv, L0_xattn_Wo,
           L0_xattn_q_norm_w, L0_xattn_k_norm_w, L0_ffn_w1q, L0_ffn_a1, L0_ffn_b1, L0_ffn_w3q, L0_ffn_a3, L0_ffn_b3,
           L0_ffn_w2q, L0_ffn_a2, L0_ffn_b2):
    import concourse.bacc as bacc
    from concourse.bass_utils import run_bass_kernel_spmd

    def arr(v):
        return np.asarray(v)

    def columns(w, n):
        return w.reshape(NC, P, n, HD).transpose(2, 1, 0, 3)

    w_qkv = arr(L0_attn_w_qkv)
    q1, k1, v1 = w_qkv[:, :G * HPG * HD], w_qkv[:, G * HPG * HD:G * (HPG + 1) * HD], w_qkv[:, G * (HPG + 1) * HD:]
    wq = np.stack([columns(q1, G * HPG), columns(arr(L0_xattn_Wq), G * HPG)]).reshape(2 * G, HPG, P, NC, HD)
    wkv = np.stack([np.concatenate([columns(k, G), columns(v, G)], axis=3)
                    for k, v in ((k1, v1), (arr(L0_xattn_Wk), arr(L0_xattn_Wv)))]).reshape(2 * G, P, NC * 2 * HD)
    wo = np.stack([arr(L0_attn_w_o), arr(L0_xattn_Wo)]).reshape(2 * G, HPG, HD, D).transpose(0, 2, 1, 3).reshape(2 * G, P, HPG * D)

    slope = ((2.0 ** (-8.0 / (G * HPG))) ** np.arange(1, G * HPG + 1, dtype=np.float32)).astype(np.float32)
    rel = np.arange(S)[:, None] - np.arange(S)[None, :]
    dist = np.sqrt(np.maximum(rel, 0).astype(np.float32))
    bias = np.where(rel[None] >= 0, -slope[:, None, None] * dist, np.float32(-1e30)).astype(np.float32)
    bias = bias.reshape(G, HPG, S, S).transpose(0, 2, 1, 3).reshape(G, S, HPG * S)

    def hidden_tiles(w):
        out = np.zeros(w.shape[:-1] + (NT, P), w.dtype)
        for k in range(NT):
            at = k // 3 * QF + k % 3 * P
            out[..., k, :KT[k % 3]] = w[..., at:at + KT[k % 3]]
        return out

    def rows(w, *places):
        out = np.zeros((4, 32, w.shape[1]), w.dtype)
        for i in places:
            out[:, 2 * i:2 * i + 2] = w
        return out.reshape(P, -1)

    def copies(*factors):
        out = np.zeros((factors[0].shape[1], 4, 32), factors[0].dtype)
        for i, f in enumerate(factors):
            out[:, :, 2 * i:2 * i + 2] = f.T[:, None, :]
        return out.reshape(-1, P)

    w13 = np.stack([hidden_tiles(arr(w).T).reshape(P, NT * P) for w in (L0_ffn_w1q, L0_ffn_w3q)])
    b13 = np.stack([rows(hidden_tiles(arr(w).T).reshape(2, NT * P), i) for i, w in enumerate((L0_ffn_b1, L0_ffn_b3))])
    b2T = rows(arr(L0_ffn_b2).T, 0, 1)
    apad = copies(arr(L0_ffn_a1), arr(L0_ffn_a3)).reshape(NC, P, P).transpose(1, 0, 2)
    a2pad = hidden_tiles(copies(arr(L0_ffn_a2), arr(L0_ffn_a2)).T).transpose(2, 1, 0)
    data = {
        "xT": arr(x).reshape(TOK, D).T.reshape(NC, P, TOK), "x": arr(x).transpose(1, 0, 2),
        "cT": arr(ctx_4096).reshape(TOK, D).T.reshape(NC, P, TOK),
        "wq": wq, "wkv": wkv, "wo": wo, "bias": bias,
        "qw": arr(L0_xattn_q_norm_w).reshape(P, 1), "kw": arr(L0_xattn_k_norm_w).reshape(P, 1),
        "w13": w13, "b13": b13, "apad": apad, "a2pad": a2pad,
        "w2T": arr(L0_ffn_w2q).T, "b2T": b2T,
    }
    data = {n: np.ascontiguousarray(v) for n, v in data.items()}
    nc = bacc.Bacc("TRN2", target_bir_lowering=False, num_devices=1)
    t = {n: nc.dram_tensor(f"in_{n}", v.shape, F32, kind="ExternalInput").ap() for n, v in data.items()}
    t["out"] = nc.dram_tensor("out", (B, S, D), F32, kind="ExternalOutput").ap()
    build(nc, t)
    r = run_bass_kernel_spmd(nc, [{f"in_{n}": v for n, v in data.items()}], core_ids=[0])
    return r.results[0]["out"]
```
